# Optimizing a Trainium2 kernel written in Bass

```python
import numpy as np
import jax
import jax.numpy as jnp

def _softmax(x, axis=-1):
    return jax.nn.softmax(x, axis=axis)

def _gelu(x):
    return jax.nn.gelu(x, approximate=True)

def _silu(x):
    return jax.nn.silu(x)

def _sigmoid(x):
    return jax.nn.sigmoid(x)

def _layernorm(x, axis=-1, eps=1e-05):
    m = jnp.mean(x, axis=axis, keepdims=True)
    v = jnp.var(x, axis=axis, keepdims=True)
    return (x - m) / jnp.sqrt(v + eps)

def _scatter_add(tgt, idx, src, axis=0):
    return tgt.at[idx].add(src)

def _segment_sum(src, seg, n):
    return jax.ops.segment_sum(src, seg, n)
kernel_name = 'mk_hybrid_d1_jaxref_r4_ea9ce1'

def setup_inputs(seed: int=0):
    np.random.seed(seed)
    _w = jnp.asarray

    def _L0_attn_a_setup():
        import jax, jax.numpy as jnp
        import numpy as np
        B_, S, H = (2, 512, 512)
        E = 2 * H
        P = 64
        NH = E // P
        N = 64
        G = 1
        K = 4
        CS = 64
        CONV_DIM = E + 2 * G * N
        PROJ = E + CONV_DIM + NH
        EPS = 1e-06

        def segment_sum(a):
            l = a.shape[-1]
            a_exp = jnp.broadcast_to(a[..., None], (*a.shape, l))
            a_exp = jnp.where(jnp.tril(jnp.ones((l, l), bool), -1), a_exp, 0.0)
            s = jnp.cumsum(a_exp, axis=-2)
            return jnp.where(jnp.tril(jnp.ones((l, l), bool), 0), s, -jnp.inf)
        key = jax.random.key(seed)
        ks = jax.random.split(key, 8)
        s = 0.02
        return {'x': jax.random.normal(ks[0], (B_, S, H), jnp.float32), 'in_proj_w': jax.random.normal(ks[1], (PROJ, H), jnp.float32) * s, 'conv_w': jax.random.normal(ks[2], (CONV_DIM, K), jnp.float32) * s, 'conv_b': jnp.zeros((CONV_DIM,), jnp.float32), 'dt_bias': jax.random.uniform(ks[3], (NH,), jnp.float32, 0.0, 1.0), 'A_log': jnp.log(jax.random.uniform(ks[4], (NH,), jnp.float32, 1.0, 16.0)), 'D': jnp.ones((NH,), jnp.float32), 'norm_w': jnp.ones((E,), jnp.float32), 'out_proj_w': jax.random.normal(ks[5], (H, E), jnp.float32) * s}
    _L0_attn_a_in = _L0_attn_a_setup()

    def _L0_attn_b_setup():
        import jax, jax.numpy as jnp
        import numpy as np
        from jax import lax
        BATCH = 2
        SEQ = 512
        HID = 512
        EXPAND = 2
        INTER = EXPAND * HID
        HEADS = 64
        PDIM = INTER // HEADS
        NSTATE = 128
        G = 1
        HPG = HEADS // G
        KCONV = 4
        GTS = G * NSTATE
        CONV_DIM = INTER + 2 * GTS
        PROJ_DIM = 2 * INTER + 2 * GTS + HEADS
        EPS = 1e-05
        MUP = (0.25, 0.5, 0.5, 0.5, 1.0)

        def _mup_vector():
            return jnp.concatenate([jnp.full((INTER,), MUP[0], jnp.float32), jnp.full((INTER,), MUP[1], jnp.float32), jnp.full((GTS,), MUP[2], jnp.float32), jnp.full((GTS,), MUP[3], jnp.float32), jnp.full((HEADS,), MUP[4], jnp.float32)])

        def _forward(hidden_states, in_proj_w, conv_w, conv_b, A_log, D, dt_bias, norm_w, out_proj_w):
            b, l, _ = hidden_states.shape
            proj = hidden_states @ in_proj_w * _mup_vector()
            z = proj[..., :INTER]
            xBC = proj[..., INTER:INTER + CONV_DIM]
            dt = proj[..., INTER + CONV_DIM:]
            xBC_cl = jnp.swapaxes(xBC, 1, 2)
            conv = lax.conv_general_dilated(xBC_cl, conv_w[:, None, :], window_strides=(1,), padding=((KCONV - 1, 0),), feature_group_count=CONV_DIM)
            xBC = jax.nn.silu(jnp.swapaxes(conv + conv_b[None, :, None], 1, 2))
            x = xBC[..., :INTER].reshape(b, l, G, HPG, PDIM)
            Bm = xBC[..., INTER:INTER + GTS].reshape(b, l, G, NSTATE)
            Cm = xBC[..., INTER + GTS:].reshape(b, l, G, NSTATE)
            dt = jax.nn.softplus(dt + dt_bias)
            A = -jnp.exp(A_log)
            dA = jnp.exp(dt * A).reshape(b, l, G, HPG)
            dtx = dt.reshape(b, l, G, HPG)[..., None] * x

            def step(state, inp):
                dA_t, dtx_t, B_t, C_t = inp
                state = state * dA_t[..., None, None] + jnp.einsum('bgcp,bgn->bgcpn', dtx_t, B_t)
                y_t = jnp.einsum('bgn,bgcpn->bgcp', C_t, state)
                return (state, y_t)
            inputs = (jnp.moveaxis(dA, 1, 0), jnp.moveaxis(dtx, 1, 0), jnp.moveaxis(Bm, 1, 0), jnp.moveaxis(Cm, 1, 0))
            state0 = jnp.zeros((b, G, HPG, PDIM, NSTATE), hidden_states.dtype)
            _, ys = lax.scan(step, state0, inputs)
            y = jnp.moveaxis(ys, 0, 1) + D.reshape(1, 1, G, HPG, 1) * x
            y = y.reshape(b, l, INTER)
            yg = y.reshape(b, l, G, INTER // G)
            var = jnp.mean(jnp.square(yg), axis=-1, keepdims=True)
            yn = (yg * lax.rsqrt(var + EPS)).reshape(b, l, INTER) * norm_w
            out = yn * jax.nn.silu(z)
            return out @ out_proj_w
        key = jax.random.key(seed)
        ks = jax.random.split(key, 8)
        hidden_states = jax.random.normal(ks[0], (BATCH, SEQ, HID), jnp.float32)
        in_proj_w = jax.random.normal(ks[1], (HID, PROJ_DIM), jnp.float32) * 0.02
        conv_w = jax.random.normal(ks[2], (CONV_DIM, KCONV), jnp.float32) * 0.2
        conv_b = jnp.zeros((CONV_DIM,), jnp.float32)
        A_log = jnp.log(jnp.arange(1, HEADS + 1, dtype=jnp.float32))
        D = jnp.ones((HEADS,), jnp.float32)
        dt_bias = jax.random.uniform(ks[3], (HEADS,), jnp.float32)
        norm_w = jnp.ones((INTER,), jnp.float32)
        out_proj_w = jax.random.normal(ks[4], (INTER, HID), jnp.float32) * 0.02
        return dict(hidden_states=hidden_states, in_proj_w=in_proj_w, conv_w=conv_w, conv_b=conv_b, A_log=A_log, D=D, dt_bias=dt_bias, norm_w=norm_w, out_proj_w=out_proj_w)
    _L0_attn_b_in = _L0_attn_b_setup()

    def _L0_ffn_setup():
        import jax, jax.numpy as jnp
        import numpy as np
        EPS = 1e-06
        K_STEPS = 4
        USE_GATING = True

        def layer_norm(x, gamma, beta):
            mu = jnp.mean(x, axis=-1, keepdims=True)
            var = jnp.mean(jnp.square(x - mu), axis=-1, keepdims=True)
            return (x - mu) * jax.lax.rsqrt(var + EPS) * gamma + beta
        key = jax.random.key(seed)
        B, L, D, H = (4, 1024, 512, 2048)
        ks = jax.random.split(key, 16)
        s = 0.02
        return {'x': jax.random.normal(ks[0], (B, L, D), dtype=jnp.float32), 'in_gamma': jnp.ones((D,), jnp.float32), 'in_beta': jnp.zeros((D,), jnp.float32), 'agg_w': jax.random.normal(ks[1], (D, D), jnp.float32) * s, 'agg_b': jnp.zeros((D,), jnp.float32), 'pn_gamma': jnp.ones((D,), jnp.float32), 'pn_beta': jnp.zeros((D,), jnp.float32), 'd1_w': jax.random.normal(ks[2], (D, H), jnp.float32) * s, 'd1_b': jnp.zeros((H,), jnp.float32), 'd2_w': jax.random.normal(ks[3], (H, D), jnp.float32) * s, 'd2_b': jnp.zeros((D,), jnp.float32), 'bc_w': jax.random.normal(ks[4], (D, D), jnp.float32) * s, 'bc_b': jnp.zeros((D,), jnp.float32), 'gate_w': jax.random.normal(ks[5], (D, D), jnp.float32) * s, 'gate_b': jnp.zeros((D,), jnp.float32), 'out_gamma': jnp.ones((D,), jnp.float32), 'out_beta': jnp.zeros((D,), jnp.float32)}
    _L0_ffn_in = _L0_ffn_setup()
    _d = {'L0_attn_a_x': _L0_attn_a_in['x'], 'L0_attn_a_in_proj_w': _L0_attn_a_in['in_proj_w'], 'L0_attn_a_conv_w': _L0_attn_a_in['conv_w'], 'L0_attn_a_conv_b': _L0_attn_a_in['conv_b'], 'L0_attn_a_dt_bias': _L0_attn_a_in['dt_bias'], 'L0_attn_a_A_log': _L0_attn_a_in['A_log'], 'L0_attn_a_D': _L0_attn_a_in['D'], 'L0_attn_a_norm_w': _L0_attn_a_in['norm_w'], 'L0_attn_a_out_proj_w': _L0_attn_a_in['out_proj_w'], 'L0_attn_b_in_proj_w': _L0_attn_b_in['in_proj_w'], 'L0_attn_b_conv_w': _L0_attn_b_in['conv_w'], 'L0_attn_b_conv_b': _L0_attn_b_in['conv_b'], 'L0_attn_b_A_log': _L0_attn_b_in['A_log'], 'L0_attn_b_D': _L0_attn_b_in['D'], 'L0_attn_b_dt_bias': _L0_attn_b_in['dt_bias'], 'L0_attn_b_norm_w': _L0_attn_b_in['norm_w'], 'L0_attn_b_out_proj_w': _L0_attn_b_in['out_proj_w'], 'L0_ffn_in_gamma': _L0_ffn_in['in_gamma'], 'L0_ffn_in_beta': _L0_ffn_in['in_beta'], 'L0_ffn_agg_w': _L0_ffn_in['agg_w'], 'L0_ffn_agg_b': _L0_ffn_in['agg_b'], 'L0_ffn_pn_gamma': _L0_ffn_in['pn_gamma'], 'L0_ffn_pn_beta': _L0_ffn_in['pn_beta'], 'L0_ffn_d1_w': _L0_ffn_in['d1_w'], 'L0_ffn_d1_b': _L0_ffn_in['d1_b'], 'L0_ffn_d2_w': _L0_ffn_in['d2_w'], 'L0_ffn_d2_b': _L0_ffn_in['d2_b'], 'L0_ffn_bc_w': _L0_ffn_in['bc_w'], 'L0_ffn_bc_b': _L0_ffn_in['bc_b'], 'L0_ffn_gate_w': _L0_ffn_in['gate_w'], 'L0_ffn_gate_b': _L0_ffn_in['gate_b'], 'L0_ffn_out_gamma': _L0_ffn_in['out_gamma'], 'L0_ffn_out_beta': _L0_ffn_in['out_beta']}
    _x0 = _d['L0_attn_a_x']
    _d['L0_attn_a_x'] = jax.random.normal(jax.random.fold_in(jax.random.key(seed), 1), (4, 1024, 512), dtype=_x0.dtype)
    del _x0
    return _d

def reference(L0_attn_a_x, L0_attn_a_in_proj_w, L0_attn_a_conv_w, L0_attn_a_conv_b, L0_attn_a_dt_bias, L0_attn_a_A_log, L0_attn_a_D, L0_attn_a_norm_w, L0_attn_a_out_proj_w, L0_attn_b_in_proj_w, L0_attn_b_conv_w, L0_attn_b_conv_b, L0_attn_b_A_log, L0_attn_b_D, L0_attn_b_dt_bias, L0_attn_b_norm_w, L0_attn_b_out_proj_w, L0_ffn_in_gamma, L0_ffn_in_beta, L0_ffn_agg_w, L0_ffn_agg_b, L0_ffn_pn_gamma, L0_ffn_pn_beta, L0_ffn_d1_w, L0_ffn_d1_b, L0_ffn_d2_w, L0_ffn_d2_b, L0_ffn_bc_w, L0_ffn_bc_b, L0_ffn_gate_w, L0_ffn_gate_b, L0_ffn_out_gamma, L0_ffn_out_beta):

    def _L0_attn_a_ref(x, in_proj_w, conv_w, conv_b, dt_bias, A_log, D, norm_w, out_proj_w):
        import jax, jax.numpy as jnp
        import numpy as np
        B_, S, H = (2, 512, 512)
        E = 2 * H
        P = 64
        NH = E // P
        N = 64
        G = 1
        K = 4
        CS = 64
        CONV_DIM = E + 2 * G * N
        PROJ = E + CONV_DIM + NH
        EPS = 1e-06

        def segment_sum(a):
            l = a.shape[-1]
            a_exp = jnp.broadcast_to(a[..., None], (*a.shape, l))
            a_exp = jnp.where(jnp.tril(jnp.ones((l, l), bool), -1), a_exp, 0.0)
            s = jnp.cumsum(a_exp, axis=-2)
            return jnp.where(jnp.tril(jnp.ones((l, l), bool), 0), s, -jnp.inf)
        b, s, _ = x.shape
        proj = x @ in_proj_w.T
        gate, hBC, dt = jnp.split(proj, [E, E + CONV_DIM], axis=-1)
        xp = jnp.pad(hBC, ((0, 0), (K - 1, 0), (0, 0)))
        conv = sum((xp[:, k:k + s, :] * conv_w[:, k] for k in range(K))) + conv_b
        hBC = jax.nn.silu(conv)
        h, Bm, Cm = jnp.split(hBC, [E, E + G * N], axis=-1)
        dt = jax.nn.softplus(dt + dt_bias)
        A = -jnp.exp(A_log)
        h = h.reshape(b, s, NH, P)
        Bm = jnp.tile(Bm.reshape(b, s, G, N), (1, 1, NH // G, 1))
        Cm = jnp.tile(Cm.reshape(b, s, G, N), (1, 1, NH // G, 1))
        pad = -s % CS
        D_res = D[:, None] * jnp.pad(h, ((0, 0), (0, pad), (0, 0), (0, 0)))
        h = h * dt[..., None]
        A_d = A * dt

        def chunk(t):
            t = jnp.pad(t, ((0, 0), (0, pad)) + ((0, 0),) * (t.ndim - 2))
            return t.reshape(b, -1, CS, *t.shape[2:])
        hc, Ac, Bc, Cc = (chunk(h), chunk(A_d), chunk(Bm), chunk(Cm))
        Ac = jnp.transpose(Ac, (0, 3, 1, 2))
        A_cs = jnp.cumsum(Ac, axis=-1)
        L = jnp.exp(segment_sum(Ac))
        Gm = jnp.einsum('bclhn,bcshn->bclsh', Cc, Bc)
        M = Gm * jnp.transpose(L, (0, 2, 3, 4, 1))
        Y_diag = jnp.einsum('bclsh,bcshp->bclhp', M, hc)
        decay = jnp.exp(A_cs[..., -1:] - A_cs)
        Bdec = Bc * jnp.transpose(decay, (0, 2, 3, 1))[..., None]
        states = jnp.einsum('bclhn,bclhp->bchpn', Bdec, hc)
        states = jnp.concatenate([jnp.zeros_like(states[:, :1]), states], axis=1)
        A_last = jnp.pad(A_cs[..., -1], ((0, 0), (0, 0), (1, 0)))
        dchunk = jnp.transpose(jnp.exp(segment_sum(A_last)), (0, 3, 2, 1))
        new_states = jnp.einsum('bzjh,bzhpn->bjhpn', dchunk, states)
        states = new_states[:, :-1]
        sdo = jnp.exp(A_cs)
        Y_off = jnp.einsum('bclhn,bchpn->bclhp', Cc, states) * jnp.transpose(sdo, (0, 2, 3, 1))[..., None]
        y = (Y_diag + Y_off).reshape(b, -1, NH, P) + D_res
        y = y[:, :s].reshape(b, s, E)
        yf = y * jax.nn.silu(gate)
        var = jnp.mean(yf * yf, axis=-1, keepdims=True)
        yn = norm_w * (yf * jax.lax.rsqrt(var + EPS))
        return yn @ out_proj_w.T

    def _L0_attn_b_ref(hidden_states, in_proj_w, conv_w, conv_b, A_log, D, dt_bias, norm_w, out_proj_w):
        import jax, jax.numpy as jnp
        import numpy as np
        from jax import lax
        BATCH = 2
        SEQ = 512
        HID = 512
        EXPAND = 2
        INTER = EXPAND * HID
        HEADS = 64
        PDIM = INTER // HEADS
        NSTATE = 128
        G = 1
        HPG = HEADS // G
        KCONV = 4
        GTS = G * NSTATE
        CONV_DIM = INTER + 2 * GTS
        PROJ_DIM = 2 * INTER + 2 * GTS + HEADS
        EPS = 1e-05
        MUP = (0.25, 0.5, 0.5, 0.5, 1.0)

        def _mup_vector():
            return jnp.concatenate([jnp.full((INTER,), MUP[0], jnp.float32), jnp.full((INTER,), MUP[1], jnp.float32), jnp.full((GTS,), MUP[2], jnp.float32), jnp.full((GTS,), MUP[3], jnp.float32), jnp.full((HEADS,), MUP[4], jnp.float32)])

        def _forward(hidden_states, in_proj_w, conv_w, conv_b, A_log, D, dt_bias, norm_w, out_proj_w):
            b, l, _ = hidden_states.shape
            proj = hidden_states @ in_proj_w * _mup_vector()
            z = proj[..., :INTER]
            xBC = proj[..., INTER:INTER + CONV_DIM]
            dt = proj[..., INTER + CONV_DIM:]
            xBC_cl = jnp.swapaxes(xBC, 1, 2)
            conv = lax.conv_general_dilated(xBC_cl, conv_w[:, None, :], window_strides=(1,), padding=((KCONV - 1, 0),), feature_group_count=CONV_DIM)
            xBC = jax.nn.silu(jnp.swapaxes(conv + conv_b[None, :, None], 1, 2))
            x = xBC[..., :INTER].reshape(b, l, G, HPG, PDIM)
            Bm = xBC[..., INTER:INTER + GTS].reshape(b, l, G, NSTATE)
            Cm = xBC[..., INTER + GTS:].reshape(b, l, G, NSTATE)
            dt = jax.nn.softplus(dt + dt_bias)
            A = -jnp.exp(A_log)
            dA = jnp.exp(dt * A).reshape(b, l, G, HPG)
            dtx = dt.reshape(b, l, G, HPG)[..., None] * x

            def step(state, inp):
                dA_t, dtx_t, B_t, C_t = inp
                state = state * dA_t[..., None, None] + jnp.einsum('bgcp,bgn->bgcpn', dtx_t, B_t)
                y_t = jnp.einsum('bgn,bgcpn->bgcp', C_t, state)
                return (state, y_t)
            inputs = (jnp.moveaxis(dA, 1, 0), jnp.moveaxis(dtx, 1, 0), jnp.moveaxis(Bm, 1, 0), jnp.moveaxis(Cm, 1, 0))
            state0 = jnp.zeros((b, G, HPG, PDIM, NSTATE), hidden_states.dtype)
            _, ys = lax.scan(step, state0, inputs)
            y = jnp.moveaxis(ys, 0, 1) + D.reshape(1, 1, G, HPG, 1) * x
            y = y.reshape(b, l, INTER)
            yg = y.reshape(b, l, G, INTER // G)
            var = jnp.mean(jnp.square(yg), axis=-1, keepdims=True)
            yn = (yg * lax.rsqrt(var + EPS)).reshape(b, l, INTER) * norm_w
            out = yn * jax.nn.silu(z)
            return out @ out_proj_w
        return _forward(hidden_states, in_proj_w, conv_w, conv_b, A_log, D, dt_bias, norm_w, out_proj_w)

    def _L0_ffn_ref(x, in_gamma, in_beta, agg_w, agg_b, pn_gamma, pn_beta, d1_w, d1_b, d2_w, d2_b, bc_w, bc_b, gate_w, gate_b, out_gamma, out_beta):
        import jax, jax.numpy as jnp
        import numpy as np
        EPS = 1e-06
        K_STEPS = 4
        USE_GATING = True

        def layer_norm(x, gamma, beta):
            mu = jnp.mean(x, axis=-1, keepdims=True)
            var = jnp.mean(jnp.square(x - mu), axis=-1, keepdims=True)
            return (x - mu) * jax.lax.rsqrt(var + EPS) * gamma + beta
        x_norm = layer_norm(x, in_gamma, in_beta)
        thought = x_norm[:, -1, :] @ agg_w + agg_b
        for _ in range(K_STEPS):
            t = layer_norm(thought, pn_gamma, pn_beta)
            t = jax.nn.gelu(t @ d1_w + d1_b, approximate=False)
            thought = thought + (t @ d2_w + d2_b)
        broadcast = (thought @ bc_w + bc_b)[:, None, :]
        if USE_GATING:
            gate = jax.nn.sigmoid(x @ gate_w + gate_b)
            out = x + gate * broadcast
        else:
            out = x + broadcast
        return layer_norm(out, out_gamma, out_beta)
    x = L0_attn_a_x
    x = x + _L0_attn_a_ref(_layernorm(x, axis=-1), L0_attn_a_in_proj_w, L0_attn_a_conv_w, L0_attn_a_conv_b, L0_attn_a_dt_bias, L0_attn_a_A_log, L0_attn_a_D, L0_attn_a_norm_w, L0_attn_a_out_proj_w)
    x = x + _L0_ffn_ref(_layernorm(x, axis=-1), L0_ffn_in_gamma, L0_ffn_in_beta, L0_ffn_agg_w, L0_ffn_agg_b, L0_ffn_pn_gamma, L0_ffn_pn_beta, L0_ffn_d1_w, L0_ffn_d1_b, L0_ffn_d2_w, L0_ffn_d2_b, L0_ffn_bc_w, L0_ffn_bc_b, L0_ffn_gate_w, L0_ffn_gate_b, L0_ffn_out_gamma, L0_ffn_out_beta)
    x = x + _L0_attn_b_ref(_layernorm(x, axis=-1), L0_attn_b_in_proj_w, L0_attn_b_conv_w, L0_attn_b_conv_b, L0_attn_b_A_log, L0_attn_b_D, L0_attn_b_dt_bias, L0_attn_b_norm_w, L0_attn_b_out_proj_w)
    x = x + _L0_ffn_ref(_layernorm(x, axis=-1), L0_ffn_in_gamma, L0_ffn_in_beta, L0_ffn_agg_w, L0_ffn_agg_b, L0_ffn_pn_gamma, L0_ffn_pn_beta, L0_ffn_d1_w, L0_ffn_d1_b, L0_ffn_d2_w, L0_ffn_d2_b, L0_ffn_bc_w, L0_ffn_bc_b, L0_ffn_gate_w, L0_ffn_gate_b, L0_ffn_out_gamma, L0_ffn_out_beta)
    return x

_drawn_inputs = setup_inputs


def setup_inputs(seed=0):
    import zlib

    import numpy as np

    out = dict(_drawn_inputs(seed))
    spreads = {'L0_attn_a_conv_b': (0.0, 0.1),
     'L0_attn_a_D': (1.0, 0.2),
     'L0_attn_a_norm_w': (1.0, 0.2),
     'L0_attn_b_conv_b': (0.0, 0.608),
     'L0_attn_b_D': (1.0, 0.6),
     'L0_attn_b_norm_w': (1.0, 0.6),
     'L0_ffn_in_gamma': (1.0, 0.2),
     'L0_ffn_in_beta': (0.0, 0.506),
     'L0_ffn_agg_b': (0.0, 0.1),
     'L0_ffn_pn_gamma': (1.0, 0.2),
     'L0_ffn_pn_beta': (0.0, 0.421),
     'L0_ffn_d1_b': (0.0, 0.1),
     'L0_ffn_d2_b': (0.0, 0.1),
     'L0_ffn_bc_b': (0.0, 0.1),
     'L0_ffn_gate_b': (0.0, 0.8),
     'L0_ffn_out_gamma': (1.0, 0.2),
     'L0_ffn_out_beta': (0.0, 0.1)}
    factors = {'L0_attn_a_dt_bias': 36.594,
     'L0_attn_a_A_log': 8.0,
     'L0_attn_b_in_proj_w': 3.412,
     'L0_attn_b_conv_w': 4.934,
     'L0_attn_b_A_log': 31.337,
     'L0_attn_b_dt_bias': 8.0,
     'L0_attn_b_out_proj_w': 3.398}
    for name, (base, spread) in spreads.items():
        noise = np.random.default_rng([zlib.crc32(name.encode()), seed]).standard_normal(out[name].shape)
        drawn = base * np.exp(spread * noise) if base else spread * noise
        out[name] = jnp.asarray(drawn.astype(out[name].dtype))
    for name, factor in factors.items():
        out[name] = (out[name] * factor).astype(out[name].dtype)
    return out
```

```python
from contextlib import ExitStack

import concourse.bass as bass
from concourse import mybir

F32 = mybir.dt.float32
F32R = mybir.dt.float32r
BF16 = mybir.dt.bfloat16
ALU = mybir.AluOpType
ACT = mybir.ActivationFunctionType

P = 128
DM = 512
KD = DM // P
E = 1024
KE = E // P
BATCH, SEQ = 4, 1024
TOK = BATCH * SEQ
SUP = 256
NSUP = TOK // SUP
SUP_PER_BATCH = SEQ // SUP
TAPS = 4
HALO = TAPS - 1
LN_EPS = 1e-5
FLOOR = -104.0
MASKED = -30000.0


FREE = 2
EXP_LN_TABLE = "natural_log_exp_and_others"
STORED = 16


def clear_signals(nc, signals):
    for s in signals:
        nc.sync.sem_clear(s)
    nc.all_engine_barrier()


class Steps:

    def __init__(self):
        self.base, self.n = 0, 0

    def next(self):
        self.n += 1
        return self.base + self.n

    def section(self, base):
        done = self.base + self.n
        self.base, self.n = base, 0
        return done


class Mixer:

    def __init__(self, tag, heads, head_dim, state, eps, gate_scale, conv_scale, gate_first):
        self.tag, self.H, self.HP, self.N = tag, heads, head_dim, state
        self.eps, self.gate_scale, self.conv_scale, self.gate_first = eps, gate_scale, conv_scale, gate_first
        self.groups = heads // 4
        self.slots = self.groups // 2
        self.chunks = max(1, self.groups // 4)
        self.blocks = [(E + b * P, P) for b in range(KE)] + [(2 * E, state), (2 * E + state, state)]
        self.dt_col = 2 * E + 2 * state
        self.proj = self.dt_col + heads


def newton_rsqrt(dve, nc, link, r, v, tmp):
    link(nc.vector.tensor_tensor(tmp, r, r, ALU.mult))
    link(nc.vector.tensor_tensor(tmp, tmp, v, ALU.mult))
    link(nc.vector.tensor_scalar(tmp, tmp, -0.5, 1.5, ALU.mult, ALU.add))
    link(nc.vector.tensor_tensor(r, r, tmp, ALU.mult))


def build_constants(nc, ctx):
    def sb(name, shape, dt=F32):
        return ctx.enter_context(nc.sbuf_tensor(name, shape, dt))

    c = {}
    c["ident"] = sb("ident", [P, P])
    c["tri_le"] = sb("tri_le", [P, P])
    c["tri_gt"] = sb("tri_gt", [P, P])
    c["ones"] = sb("ones", [P, P])
    c["mean_w"] = sb("mean_w", [P, P])
    c["ident_bf"] = sb("ident_bf", [P, P], BF16)
    c["masked_bf"] = sb("masked_bf", [P, 4, P], BF16)
    c["in_group"] = sb("in_group", [P, 16])
    c["in_head"] = sb("in_head", [P, 4])
    c["keep"] = sb("keep", [P, NSUP + 1])
    c["lhs"] = [sb("lhs_hi", [P, 16, P], F32R), sb("lhs_lo", [P, 16, P], F32R)]
    c["rhs"] = [sb("rhs_hi", [P, 4, P], F32R), sb("rhs_lo", [P, 4, P], F32R)]
    grp = sb("grp", [P, 2, 16])
    hd = sb("hd", [P, 4, 32])
    made, built = (ctx.enter_context(nc.semaphore(n)) for n in ("const_made", "const_built"))
    with nc.Block() as block:
        @block.gpsimd
        def _(pool):
            k = [0]

            def step(ins):
                ins.then_inc(made, 1)
                k[0] += 1
                pool.wait_ge(made, k[0])

            for t, v in (("ident", 0.0), ("tri_le", 1.0), ("tri_gt", 1.0), ("ones", 1.0), ("mean_w", 1.0 / DM),
                         ("ident_bf", 0.0), ("masked_bf", 0.0), ("keep", 1.0)):
                step(nc.gpsimd.memset(c[t][:], v))
            step(nc.gpsimd.memset(grp[:], 1.0))
            step(nc.gpsimd.memset(hd[:], 0.0))
            step(nc.gpsimd.affine_select(out=c["ident"][:], in_=c["ident"][:], compare_op=ALU.not_equal, fill=1.0,
                                         base=0, pattern=[[-1, P]], channel_multiplier=1))
            step(nc.gpsimd.affine_select(out=c["ident_bf"][:], in_=c["ident_bf"][:], compare_op=ALU.not_equal,
                                         fill=1.0, base=0, pattern=[[-1, P]], channel_multiplier=1))
            step(nc.gpsimd.affine_select(out=c["tri_le"][:], in_=c["tri_le"][:], compare_op=ALU.is_ge, fill=0.0,
                                         base=0, pattern=[[1, P]], channel_multiplier=-1))
            step(nc.gpsimd.affine_select(out=c["tri_gt"][:], in_=c["tri_gt"][:], compare_op=ALU.is_gt, fill=0.0,
                                         base=0, pattern=[[-1, P]], channel_multiplier=1))
            step(nc.gpsimd.affine_select(out=c["masked_bf"][:], in_=c["masked_bf"][:], compare_op=ALU.is_ge,
                                         fill=MASKED, base=0, pattern=[[0, 4], [1, P]], channel_multiplier=-1))
            step(nc.gpsimd.affine_select(out=grp[:], in_=grp[:], compare_op=ALU.is_ge, fill=0.0,
                                         base=0, pattern=[[-64, 2], [-4, 16]], channel_multiplier=1))
            step(nc.gpsimd.affine_select(out=grp[:], in_=grp[:], compare_op=ALU.is_ge, fill=0.0,
                                         base=3, pattern=[[64, 2], [4, 16]], channel_multiplier=-1))
            step(nc.gpsimd.affine_select(out=hd[:], in_=hd[:], compare_op=ALU.not_equal, fill=1.0,
                                         base=0, pattern=[[-1, 4], [-4, 32]], channel_multiplier=1))
            for b in range(BATCH):
                step(nc.gpsimd.memset(c["keep"][:, b * SUP_PER_BATCH:b * SUP_PER_BATCH + 1], 0.0))
            c["steps"] = k[0]

        @block.vector
        def _(dve):
            dve.wait_ge(made, c["steps"])
            nc.vector.tensor_tensor(c["in_group"][:], grp[:, 0], grp[:, 1], ALU.add).then_inc(built, 1)
            nc.vector.tensor_reduce(c["in_head"][:], hd[:], mybir.AxisListType.X, ALU.add).then_inc(built, 1)
            dve.wait_ge(built, 2)
            for part in range(2):
                nc.vector.tensor_copy(c["lhs"][part][0:64], c["in_group"][0:64].unsqueeze(2).to_broadcast([64, 16, P])
                                      ).then_inc(built, 1)
                nc.vector.tensor_copy(c["rhs"][part][64:P], c["in_head"][64:P].unsqueeze(2).to_broadcast([64, 4, P])
                                      ).then_inc(built, 1)
            dve.wait_ge(built, 6)
    return c


def mixer_phase(nc, cfg, c, mem, psum, x_src, x_dst, w):
    H, HP, N, NS, G = cfg.H, cfg.HP, cfg.N, cfg.slots, cfg.groups
    NB = len(cfg.blocks)
    CHG = G // cfg.chunks
    ident, tri_le, tri_gt, ones = c["ident"], c["tri_le"], c["tri_gt"], c["ones"]
    xs_src = x_src.rearrange("(s j p) d -> s p j d", p=P, j=2)
    xs_dst = x_dst.rearrange("(s j p) d -> s p j d", p=P, j=2)

    ctx = ExitStack()
    with ctx:
        def sb(name, shape, dt=F32):
            return ctx.enter_context(nc.sbuf_tensor(f"{cfg.tag}_{name}", shape, dt))

        signals = []

        def sig(name):
            signals.append(ctx.enter_context(nc.semaphore(f"{cfg.tag}_{name}")))
            return signals[-1]

        w_in = sb("w_in", [P, KD, cfg.proj])
        w_out = sb("w_out", [P, KE, DM])
        conv_w = sb("conv_w", [P, NB, TAPS])
        conv_b = sb("conv_b", [P, NB])
        norm_w = sb("norm_w", [P, KE])
        dt_bias = sb("dt_bias", [P, H])
        a_log = sb("a_log", [P, H])
        a_low, a_high = sb("a_low", [P, H]), sb("a_high", [P, H])
        d_skip = sb("d_skip", [P, H])
        x_in = sb("x_in", [P, 2, DM])
        x_res = sb("x_res", [P, 2, DM])
        stats = sb("stats", [P, 2, 6])
        mv = sb("mv", [P, 2, 2])
        ln_v, ln_r, ln_t = sb("ln_v", [P, 2]), sb("ln_r", [P, 2]), sb("ln_t", [P, 2])
        xn = sb("xn", [P, 2, DM])
        xnT = sb("xnT", [P, KD, SUP])
        pre = sb("pre", [P, NB, HALO + SUP])
        cv = sb("cv", [P, NB, SUP])
        xs = sb("xs", [P, KE, SUP])
        bcs = sb("bcs", [P, 2, SUP])
        z_raw = sb("z_raw", [P, 2, E])
        zs = sb("zs", [P, 2, E])
        raw, sp_e = sb("raw", [P, 2, H]), sb("sp_e", [P, 2, H])
        dt = sb("dt", [P, 2, H])
        a_step = sb("a_step", [P, 2, H])
        aa = sb("aa", [P, 2, P])
        xt = sb("xt", [P, 2, E])
        bt = sb("bt", [P, 2, N])
        xdt = sb("xdt", [P, 2, E])
        cs3 = sb("cs3", [P, 3, H])
        e3 = sb("e3", [P, 3, H])
        gt = sb("gt", [P, P])
        hi, lo = sb("hi", [P, P], F32R), sb("lo", [P, P], F32R)
        decay = sb("decay", [P, 2, 8, P])
        y1 = sb("y1", [P, E])
        skip = sb("skip", [P, E])
        xw = sb("xw", [P, E])
        state = sb("state", [P, E])
        yy, yz = sb("yy", [P, E]), sb("yz", [P, E])
        yzT = sb("yzT", [P, KE, P])
        ss = sb("ss", [P, 1])
        rv, rr, rt = sb("rv", [P, 1]), sb("rr", [P, 1]), sb("rt", [P, 1])

        kcol = sb("kcol", [P, 1])
        carrier = sb("carrier", [P, 1])

        work, seg, ybank = psum["work"], psum["seg"], psum["y"]

        weights = sig("weights")
        setup_v = sig("setup_v")
        setup_a = sig("setup_a")
        x_loaded = sig("x_loaded")
        res_loaded = sig("res_loaded")
        stored = sig("stored")
        v_chain = sig("v_chain")
        a_chain = sig("a_chain")
        p_chain = sig("p_chain")
        var_ready = sig("var_ready")
        r0_ready = sig("r0_ready")
        xn_ready = sig("xn_ready")
        work_full = sig("work_full")
        xnT_ready = sig("xnT_ready")
        raw_ready = sig("raw_ready")
        nabs_ready = sig("nabs_ready")
        sp_ready = sig("sp_ready")
        tap_ready = sig("tap_ready")
        conv_done = sig("conv_done")
        halo_done = sig("halo_done")
        z_ready = sig("z_ready")
        silu_done = sig("silu_done")
        zs_done = sig("zs_done")
        xt_ready = sig("xt_ready")
        bt_ready = sig("bt_ready")
        aa_ready = sig("aa_ready")
        xdt_done = sig("xdt_done")
        cs3_ready = sig("cs3_ready")
        hilo_ready = sig("hilo_ready")
        rhs_ready = sig("rhs_ready")
        lhs_ready = sig("lhs_ready")
        e3_ready = sig("e3_ready")
        kcol_ready = sig("kcol_ready")
        kept = sig("kept")
        y1_ready = sig("y1_ready")
        y1x_ready = sig("y1x_ready")
        xw_ready = sig("xw_ready")
        dec_done = sig("dec_done")
        state_ready = sig("state_ready")
        seg_full = sig("seg_full")
        exp_done = sig("exp_done")
        m_ready = sig("m_ready")
        ydiag_done = sig("ydiag_done")
        yy_done = sig("yy_done")
        yz_done = sig("yz_done")
        sq_done = sig("sq_done")
        rv_ready = sig("rv_ready")
        r1_ready = sig("r1_ready")
        yzT_ready = sig("yzT_ready")
        out_done = sig("out_done")

        pro_uses = (["xnT0", "xnT1", "dt"] + [f"blk{b}" for b in range(NB)] + [f"z{k}" for k in range(4)]
                    + [f"xT{k}" for k in range(4)] + ["BT"])
        tile_end = ["yT{j}a", "yT{j}b", "out{j}"]
        fill0 = ["xnT0", "xnT1", "dt"] + [f"blk{b}" for b in range(NB)]

        def spread(names, slots):
            return [names[len(names) * s // slots:len(names) * (s + 1) // slots] for s in range(slots)]

        def schedule(with_next):
            steps = ["small0"] + (["xnT0", "xnT1", "dt"] if with_next else []) + ["yoff0a", "yoff0b"]
            fill = spread(fill0[3:], NS) if with_next else [[]] * NS
            for s in range(NS):
                steps += [f"seg0.{s}"] + fill[s] + ([f"ydiag0.{s - 1}"] if s else [])
            steps += ["state0a", "state0b", "small1", f"ydiag0.{NS - 1}", "yT0a", "yT0b", "out0",
                      "yoff1a", "yoff1b"]
            for s in range(NS):
                steps += [f"seg1.{s}"] + ([f"ydiag1.{s - 1}"] if s else [])
            steps += ["state1a", "state1b", f"ydiag1.{NS - 1}"]
            if with_next:
                steps += [f"z{k}" for k in range(4)]
            steps += ["yT1a", "yT1b", "out1"]
            if with_next:
                steps += [f"xT{k}" for k in range(4)] + ["BT"]
            return steps

        def is_use(step):
            return not step.startswith(("seg", "ydiag"))

        loop_uses = [s for s in schedule(True) if is_use(s)]
        last_uses = [s for s in schedule(False) if is_use(s)]
        assert len(pro_uses) % 2 == 0 and len(loop_uses) % 2 == 0 and len(last_uses) % 2 == 0
        assert pro_uses[-2:] == loop_uses[-2:]

        class Section:

            def __init__(self, uses, base, i, n, ln=None):
                self.uses, self.base, self.i, self.n = uses, base, i, n
                self.ln = ln

            def full(self, name):
                return self.base + self.uses.index(name) + 1

            def bank(self, name):
                return work[self.uses.index(name) % 2]

        def prologue():
            return Section(pro_uses, 0, None, 0, 1)

        def body(i):
            return Section(loop_uses, i * len(loop_uses) + len(pro_uses), i, i + 1, i + 2)

        def last_but_one():
            i = NSUP - 2
            return Section(loop_uses, i * len(loop_uses) + len(pro_uses), i, i + 1)

        def last():
            i = NSUP - 1
            return Section(last_uses, i * len(loop_uses) + len(pro_uses), i, None)

        def freed(eng, name, i, n):
            if name[:3] == "xnT":
                eng.wait_ge(xnT_ready, FREE + n * 2 + int(name[3]) + 1)
            elif name == "dt":
                eng.wait_ge(raw_ready, FREE + n + 1)
            elif name[:3] == "blk":
                eng.wait_ge(tap_ready, FREE + n * NB + int(name[3:]) + 1)
            elif name[0] == "z":
                eng.wait_ge(z_ready, FREE + n * 4 + int(name[1]) + 1)
            elif name[:2] == "xT":
                eng.wait_ge(xt_ready, FREE + n * 4 + int(name[2]) + 1)
            elif name == "BT":
                eng.wait_ge(bt_ready, FREE + n + 1)
            elif name[:5] == "small":
                eng.wait_ge(hilo_ready, FREE + i * 2 + int(name[5]) + 1)
            elif name[:4] == "yoff":
                eng.wait_ge(y1_ready, FREE + i * 4 + 2 * int(name[4]) + "ab".index(name[5]) + 1)
            elif name[:5] == "state":
                eng.wait_ge(state_ready, FREE + i * 4 + 2 * int(name[5]) + "ab".index(name[6]) + 1)
            elif name[:2] == "yT":
                eng.wait_ge(yzT_ready, FREE + i * 4 + 2 * int(name[2]) + "ab".index(name[3]) + 1)
            elif name[:3] == "out":
                eng.wait_ge(out_done, FREE + i * 2 + int(name[3]) + 1)
            else:
                raise ValueError(name)

        with nc.Block() as block:
            @block.sync
            def _(sp):
                sp.sem_inc(stored, STORED)
                sp.dma_start(x_in[:], xs_src[0]).then_inc(x_loaded, 16)
                n_w = [0]

                def load(dst, src):
                    sp.dma_start(dst, src).then_inc(weights, 16)
                    n_w[0] += 16

                load(w_in[:], w["in_proj"].rearrange("(t p) n -> p t n", p=P))
                with nc.allow_non_contiguous_dma(reason="small vectors"):
                    for b, (col, m) in enumerate(cfg.blocks):
                        load(conv_w[0:m, b, :], w["conv_w"][col - E:col - E + m, :])
                        load(conv_b[0:m, b:b + 1], w["conv_b"][col - E:col - E + m].rearrange("(p a) -> p a", a=1))
                    load(norm_w[:], w["norm_w"].rearrange("(k p) -> p k", p=P))
                for dst, name in ((dt_bias, "dt_bias"), (a_log, "A_log"), (d_skip, "D")):
                    load(dst[:], w[name].rearrange("(a h) -> a h", a=1).to_broadcast([P, H]))
                load(w_out[:], w["out_proj"].rearrange("(k p) n -> p k n", p=P))
                cfg.weight_count = n_w[0]

                def load_x(m):
                    sp.wait_ge(xn_ready, FREE + 2 * m)
                    sp.dma_start(x_in[:], xs_src[m]).then_inc(x_loaded, 16)

                def step(i, m):
                    if m is not None:
                        load_x(m)
                    sp.wait_ge(stored, STORED + 16 * i)
                    sp.dma_start(x_res[:], xs_src[i]).then_inc(res_loaded, 16)
                    sp.wait_ge(out_done, FREE + 2 * i + 2)
                    sp.dma_start(xs_dst[i], x_res[:]).then_inc(stored, 16)

                load_x(1)
                with sp.Fori(0, NSUP - 2) as i:
                    step(i, i + 2)
                step(NSUP - 2, None)
                step(NSUP - 1, None)
                sp.wait_ge(stored, STORED + 16 * NSUP)

            @block.tensor
            def _(pe):
                def project(dst, col, m, sec):
                    for k in range(KD):
                        mm = nc.tensor.matmul(dst, w_in[:, k, col:col + m], xnT[:, k, :],
                                              start=(k == 0), stop=(k == KD - 1))
                    return mm

                def use(name, sec):
                    i, n = sec.i, sec.n
                    idx = sec.uses.index(name)
                    if idx >= 2:
                        freed(pe, sec.uses[idx - 2], i, n)
                    elif i is not None:
                        freed(pe, loop_uses[idx - 2], None, i)
                    bank = sec.bank(name)
                    if name[:3] == "xnT":
                        j = int(name[3])
                        pe.wait_ge(xn_ready, FREE + 2 * n + j + 1)
                        for k in range(KD):
                            mm = nc.tensor.transpose(bank[:, k * P:(k + 1) * P], xn[:, j, k * P:(k + 1) * P], ident[:])
                    elif name == "dt":
                        pe.wait_ge(xnT_ready, FREE + 2 * n + 2)
                        for j in range(2):
                            for k in range(KD):
                                mm = nc.tensor.matmul(bank[:, j * H:(j + 1) * H], xnT[:, k, j * P:(j + 1) * P],
                                                      w_in[:, k, cfg.dt_col:cfg.dt_col + H],
                                                      start=(k == 0), stop=(k == KD - 1))
                    elif name[:3] == "blk":
                        col, m = cfg.blocks[int(name[3:])]
                        mm = project(bank[0:m, 0:SUP], col, m, sec)
                    elif name[0] == "z":
                        j, half = divmod(int(name[1]), 2)
                        for k in range(KD):
                            mm = nc.tensor.matmul(bank[:, :], xnT[:, k, j * P:(j + 1) * P],
                                                  w_in[:, k, half * 512:(half + 1) * 512],
                                                  start=(k == 0), stop=(k == KD - 1))
                    elif name[:2] == "xT":
                        j, half = divmod(int(name[2]), 2)
                        pe.wait_ge(silu_done, FREE + 2 * n + 1)
                        for q in range(4):
                            mm = nc.tensor.transpose(bank[:, q * P:(q + 1) * P],
                                                     xs[:, half * 4 + q, j * P:(j + 1) * P], ident[:])
                    elif name == "BT":
                        pe.wait_ge(silu_done, FREE + 2 * n + 2)
                        for j in range(2):
                            mm = nc.tensor.matmul(bank[:, j * N:(j + 1) * N], bcs[0:N, 0, j * P:(j + 1) * P],
                                                  ident[0:N, 0:N], start=True, stop=True)
                    elif name[:5] == "small":
                        j = int(name[5])
                        pe.wait_ge(aa_ready, i + 1)
                        pe.wait_ge(silu_done, FREE + 2 * i + 2)
                        nc.tensor.matmul(bank[:, 0:H], tri_le[:], aa[:, j, 0:H], start=True, stop=True)
                        nc.tensor.matmul(bank[:, H:2 * H], tri_gt[:], aa[:, j, 0:H], start=True, stop=True)
                        nc.tensor.matmul(bank[:, 2 * H:3 * H], ones[:], aa[:, j, 0:H], start=True, stop=True)
                        nc.tensor.matmul(bank[:, 192:320], aa[:, j, :], tri_le[:], start=True, stop=True)
                        mm = nc.tensor.matmul(bank[:, 320:448], bcs[0:N, 0, j * P:(j + 1) * P],
                                              bcs[0:N, 1, j * P:(j + 1) * P], start=True, stop=True)
                    elif name[:4] == "yoff":
                        j, q = int(name[4]), "ab".index(name[5])
                        pe.wait_ge(state_ready, FREE + 2 * (2 * i + j))
                        mm = nc.tensor.matmul(bank[:, :], bcs[0:N, 1, j * P:(j + 1) * P],
                                              state[0:N, q * 512:(q + 1) * 512], start=True, stop=True)
                    elif name[:5] == "state":
                        j, q = int(name[5]), "ab".index(name[6])
                        pe.wait_ge(xw_ready, FREE + 2 * i + j + 1)
                        mm = nc.tensor.matmul(bank[0:N, :], bt[:, j, :], xw[:, q * 512:(q + 1) * 512],
                                              start=True, stop=True)
                    elif name[:2] == "yT":
                        j, q = int(name[2]), "ab".index(name[3])
                        pe.wait_ge(yz_done, FREE + 2 * i + j + 1)
                        for b in range(4):
                            mm = nc.tensor.transpose(bank[:, b * P:(b + 1) * P],
                                                     yz[:, (q * 4 + b) * P:(q * 4 + b + 1) * P], ident[:])
                    else:
                        j = int(name[3])
                        pe.wait_ge(yzT_ready, FREE + 2 * (2 * i + j) + 2)
                        for k in range(KE):
                            mm = nc.tensor.matmul(bank[:, :], yzT[:, k, :], w_out[:, k, :],
                                                  start=(k == 0), stop=(k == KE - 1))
                    mm.then_inc(work_full, 1)

                def seg_slot(tile, s):
                    pe.wait_ge(lhs_ready, FREE + tile * cfg.chunks + (2 * s + 1) // CHG + 1)
                    pe.wait_ge(rhs_ready, tile + 1)
                    pe.wait_ge(exp_done, FREE + tile * NS + s - 1)
                    for q in range(2):
                        g = 2 * s + q
                        dst = seg[s % 2][:, q * 512:(q + 1) * 512]
                        for part in range(2):
                            nc.tensor.matmul(dst, c["lhs"][part][:, g, :],
                                             c["rhs"][part][:].rearrange("p h l -> p (h l)"),
                                             start=(part == 0), stop=False)
                        mm = nc.tensor.matmul(dst, c["ident_bf"][:], c["masked_bf"][:].rearrange("p h l -> p (h l)"),
                                              start=False, stop=True)
                    mm.then_inc(seg_full, 1)

                def ydiag_slot(tile, j, s):
                    pe.wait_ge(m_ready, tile * NS + s + 1)
                    if s == 0:
                        pe.wait_ge(yy_done, FREE + tile)
                    for h in range(8):
                        head = 8 * s + h
                        mm = nc.tensor.matmul(ybank[:, head * HP:(head + 1) * HP], decay[:, s % 2, h, :],
                                              xdt[:, j, head * HP:(head + 1) * HP], start=True, stop=True)
                    mm.then_inc(ydiag_done, 1)

                def run(sec, steps):
                    for name in steps:
                        if is_use(name):
                            use(name, sec)
                        else:
                            kind, s = name.split(".")
                            j = int(kind[-1])
                            if kind[:3] == "seg":
                                seg_slot(2 * sec.i + j, int(s))
                            else:
                                if s == "0":
                                    pe.wait_ge(xdt_done, FREE + 2 * sec.i + j + 1)
                                ydiag_slot(2 * sec.i + j, j, int(s))

                pe.sem_inc(ydiag_done, FREE)
                pe.wait_ge(weights, cfg.weight_count)
                pe.wait_ge(setup_v, 3)
                run(prologue(), pro_uses)
                with pe.Fori(0, NSUP - 2) as i:
                    run(body(i), schedule(True))
                run(last_but_one(), schedule(True))
                run(last(), schedule(False))

            @block.scalar
            def _(act):
                steps = Steps()

                def link(ins):
                    ins.then_inc(a_chain, 1)
                    act.wait_ge(a_chain, steps.next())

                def norm_rsqrt(m):
                    act.wait_ge(var_ready, m + 1)
                    link(nc.scalar.activation(ln_r[:], ln_v[:], ACT.Ln))
                    nc.scalar.activation(ln_r[:], ln_r[:], ACT.Exp, scale=-0.5).then_inc(r0_ready, 1)

                def xnT_copy(sec, j):
                    act.wait_ge(work_full, sec.full(f"xnT{j}"))
                    nc.scalar.copy(xnT[:, :, j * P:(j + 1) * P],
                                   sec.bank(f"xnT{j}")[:, :].rearrange("p (k t) -> p k t", k=KD)
                                   ).then_inc(xnT_ready, 1)

                def softplus(sec):
                    act.wait_ge(nabs_ready, sec.n + 1)
                    link(nc.scalar.activation(sp_e[:], sp_e[:], ACT.Exp))
                    nc.scalar.activation(sp_e[:], sp_e[:], ACT.Ln, bias=1.0).then_inc(sp_ready, 1)

                def block_copy(sec, b):
                    m = cfg.blocks[b][1]
                    act.wait_ge(work_full, sec.full(f"blk{b}"))
                    if b == 0:
                        act.wait_ge(halo_done, FREE + sec.n)
                    bank = sec.bank(f"blk{b}")
                    nc.scalar.copy(pre[0:m, b, HALO:], bank[0:m, 0:SUP])
                    nc.scalar.activation(cv[0:m, b, :], bank[0:m, 0:SUP], ACT.Identity, bias=conv_b[0:m, b:b + 1],
                                         scale=conv_w[0:m, b, TAPS - 1:TAPS]).then_inc(tap_ready, 1)

                def z_copy(sec, k):
                    j, half = divmod(k, 2)
                    act.wait_ge(work_full, sec.full(f"z{k}"))
                    nc.scalar.copy(z_raw[:, j, half * 512:(half + 1) * 512], sec.bank(f"z{k}")[:, :]
                                   ).then_inc(z_ready, 1)

                def silus(sec):
                    n = sec.n
                    act.wait_ge(conv_done, FREE + (n + 1) * NB)
                    act.wait_ge(xt_ready, FREE + 4 * n)
                    nc.scalar.activation(xs[:], cv[:, 0:KE, :], ACT.Silu).then_inc(silu_done, 1)
                    act.wait_ge(y1_ready, FREE + 4 * n)
                    nc.scalar.activation(bcs[0:N], cv[0:N, KE:NB, :], ACT.Silu).then_inc(silu_done, 1)
                    act.wait_ge(z_ready, FREE + 4 * n + 4)
                    act.wait_ge(yz_done, FREE + 2 * n)
                    nc.scalar.activation(zs[:], z_raw[:], ACT.Silu, scale=cfg.gate_scale
                                         ).then_inc(zs_done, 1)
                    nc.scalar.preload_act_table_set(EXP_LN_TABLE)

                def xt_copy(sec, k):
                    j, half = divmod(k, 2)
                    act.wait_ge(work_full, sec.full(f"xT{k}"))
                    if k == 0:
                        act.wait_ge(y1x_ready, FREE + 2 * sec.n)
                        act.wait_ge(xdt_done, FREE + 2 * sec.n)
                    nc.scalar.copy(xt[:, j, half * 512:(half + 1) * 512], sec.bank(f"xT{k}")[:, :]
                                   ).then_inc(xt_ready, 1)

                def bt_copy(sec):
                    act.wait_ge(work_full, sec.full("BT"))
                    act.wait_ge(state_ready, FREE + 4 * sec.n)
                    nc.scalar.copy(bt[:].rearrange("p j n -> p (j n)"), sec.bank("BT")[:, 0:2 * N]
                                   ).then_inc(bt_ready, 1)

                def sums_exp(sec, j):
                    tile = 2 * sec.i + j
                    act.wait_ge(cs3_ready, tile + 1)
                    act.wait_ge(dec_done, FREE + tile)
                    act.wait_ge(y1_ready, FREE + 2 * tile)
                    nc.scalar.activation(e3[:], cs3[:], ACT.Exp).then_inc(e3_ready, 1)

                def slot_exp(sec, j, s):
                    u = (2 * sec.i + j) * NS + s
                    act.wait_ge(seg_full, u + 1)
                    act.wait_ge(ydiag_done, FREE + u - 1)
                    nc.scalar.activation(decay[:, s % 2].rearrange("p h l -> p (h l)"), seg[s % 2][:, :], ACT.Exp
                                         ).then_inc(exp_done, 1)

                def square(sec, j):
                    tile = 2 * sec.i + j
                    src = yz if cfg.gate_first else yy
                    if cfg.gate_first:
                        act.wait_ge(yz_done, FREE + tile + 1)
                    else:
                        act.wait_ge(yy_done, FREE + tile + 1)
                    act.wait_ge(rv_ready, FREE + tile)
                    act.wait_ge(y1x_ready, FREE + tile + 1)
                    nc.scalar.activation(skip[:], src[:], ACT.Square, accum_out=ss[:]).then_inc(sq_done, 1)

                def out_rsqrt(sec, j):
                    tile = 2 * sec.i + j
                    act.wait_ge(rv_ready, FREE + tile + 1)
                    act.wait_ge(out_done, FREE + tile)
                    link(nc.scalar.activation(rr[:], rv[:], ACT.Ln))
                    nc.scalar.activation(rr[:], rr[:], ACT.Exp, scale=-0.5).then_inc(r1_ready, 1)

                def yzT_copy(sec, j, q):
                    tile = 2 * sec.i + j
                    name = f"yT{j}" + "ab"[q]
                    act.wait_ge(work_full, sec.full(name))
                    act.wait_ge(out_done, FREE + tile)
                    nc.scalar.copy(yzT[:, q * 4:(q + 1) * 4, :],
                                   sec.bank(name)[:, :].rearrange("p (k t) -> p k t", k=4)
                                   ).then_inc(yzT_ready, 1)

                def tile_steps(sec, j, fill):
                    sums_exp(sec, j)
                    for s in range(NS):
                        slot_exp(sec, j, s)
                        for b in fill[s]:
                            block_copy(sec, b)

                def tile_finish(sec, j):
                    yzT_copy(sec, j, 0)
                    yzT_copy(sec, j, 1)
                    square(sec, j)
                    out_rsqrt(sec, j)

                def supertile(sec, with_next):
                    if with_next:
                        xnT_copy(sec, 0)
                        xnT_copy(sec, 1)
                        softplus(sec)
                        fill = spread(list(range(NB)), NS)
                    else:
                        fill = [[]] * NS
                    tile_steps(sec, 0, fill)
                    tile_finish(sec, 0)
                    tile_steps(sec, 1, [[]] * NS)
                    if with_next:
                        for k in range(4):
                            z_copy(sec, k)
                    tile_finish(sec, 1)
                    if sec.ln is not None:
                        norm_rsqrt(sec.ln)
                    if with_next:
                        silus(sec)
                        for k in range(4):
                            xt_copy(sec, k)
                        bt_copy(sec)

                for s in (xnT_ready, tap_ready, z_ready, silu_done, zs_done, xt_ready, bt_ready, exp_done, sq_done, e3_ready,
                          yzT_ready):
                    act.sem_inc(s, FREE)
                nc.scalar.preload_act_table_set(EXP_LN_TABLE)
                act.wait_ge(weights, cfg.weight_count)
                act.wait_ge(setup_v, 1)
                nc.scalar.activation(a_low[:], a_low[:], ACT.Exp)
                nc.scalar.activation(a_high[:], a_high[:], ACT.Exp).then_inc(setup_a, 1)
                act.wait_ge(setup_v, 3)
                sec = prologue()
                norm_rsqrt(0)
                xnT_copy(sec, 0)
                xnT_copy(sec, 1)
                softplus(sec)
                for b in range(NB):
                    block_copy(sec, b)
                for k in range(4):
                    z_copy(sec, k)
                norm_rsqrt(1)
                silus(sec)
                for k in range(4):
                    xt_copy(sec, k)
                bt_copy(sec)
                per = 4
                base = steps.section(0)
                with act.Fori(0, NSUP - 2) as i:
                    steps.section(i * per + base)
                    supertile(body(i), True)
                    assert steps.n == per, steps.n
                steps.section((NSUP - 2) * per + base)
                supertile(last_but_one(), True)
                supertile(last(), False)

            @block.vector
            def _(dve):
                steps = Steps()

                def link(ins):
                    ins.then_inc(v_chain, 1)
                    dve.wait_ge(v_chain, steps.next())

                def norm_stats(n):
                    dve.wait_ge(x_loaded, 16 * n + 16)
                    nc.vector.bn_stats(stats[:, 0, :], x_in[:, 0, :])
                    link(nc.vector.bn_stats(stats[:, 1, :], x_in[:, 1, :]))
                    nc.vector.memset(carrier[:], 0.0)
                    nc.vector.bn_aggr(mv[:, 0, :], stats[:, 0, :])
                    link(nc.vector.bn_aggr(mv[:, 1, :], stats[:, 1, :]))
                    nc.vector.tensor_scalar(ln_v[:], mv[:, :, 1], LN_EPS, None, ALU.add).then_inc(var_ready, 1)

                def norm_apply(n):
                    dve.wait_ge(r0_ready, n + 1)
                    newton_rsqrt(dve, nc, link, ln_r[:], ln_v[:], ln_t[:])
                    dve.wait_ge(xnT_ready, FREE + 2 * n)
                    for j in range(2):
                        nc.vector.tensor_scalar(xn[:, j, :], x_in[:, j, :], mv[:, j, 0:1], ln_r[:, j:j + 1],
                                                ALU.subtract, ALU.mult).then_inc(xn_ready, 1)

                def dt_raw(sec):
                    dve.wait_ge(work_full, sec.full("dt"))
                    nc.vector.tensor_tensor(raw[:], sec.bank("dt")[:, 0:2 * H].rearrange("p (j h) -> p j h", j=2),
                                            dt_bias[:].unsqueeze(1).to_broadcast([P, 2, H]), ALU.add
                                            ).then_inc(raw_ready, 1)
                    dve.wait_ge(raw_ready, FREE + sec.n + 1)
                    nc.vector.scalar_tensor_tensor(out=sp_e[:], in0=raw[:], scalar=-1.0, in1=raw[:],
                                                   op0=ALU.mult, op1=ALU.min).then_inc(nabs_ready, 1)

                def dt_finish(sec):
                    dve.wait_ge(sp_ready, sec.n + 1)
                    link(nc.vector.scalar_tensor_tensor(out=dt[:], in0=raw[:], scalar=0.0, in1=sp_e[:],
                                                        op0=ALU.max, op1=ALU.add))
                    link(nc.vector.tensor_tensor(a_step[:], dt[:], a_low[:].unsqueeze(1).to_broadcast([P, 2, H]),
                                                 ALU.mult))
                    link(nc.vector.tensor_scalar(a_step[:], a_step[:], -1.0, FLOOR, ALU.mult, ALU.max))
                    link(nc.vector.tensor_tensor(a_step[:], a_step[:], a_high[:].unsqueeze(1).to_broadcast([P, 2, H]),
                                                 ALU.mult))

                def conv_blocks(sec, pair):
                    dve.wait_ge(tap_ready, FREE + sec.n * NB + pair[-1] + 1)
                    for t in range(HALO):
                        for b in pair:
                            m = cfg.blocks[b][1]
                            ins = nc.vector.scalar_tensor_tensor(
                                out=cv[0:m, b, :], in0=pre[0:m, b, t:t + SUP], scalar=conv_w[0:m, b, t:t + 1],
                                in1=cv[0:m, b, :], op0=ALU.mult, op1=ALU.add)
                            if t == HALO - 1:
                                ins.then_inc(conv_done, 1)
                            else:
                                ins.then_inc(v_chain, 1)
                                taps_count = steps.next()
                        if t < HALO - 1:
                            dve.wait_ge(v_chain, taps_count)

                def halo(sec):
                    dve.wait_ge(conv_done, FREE + (sec.n + 1) * NB)
                    nx = sec.n + 1
                    k = c["keep"][:, nx:nx + 1] if isinstance(nx, int) else c["keep"][:, bass.ds(nx, 1)]
                    nc.vector.tensor_scalar(pre[:, 0:KE, 0:HALO], pre[:, 0:KE, SUP:SUP + HALO], k, None, ALU.mult)
                    kn = c["keep"][0:N, nx:nx + 1] if isinstance(nx, int) else c["keep"][0:N, bass.ds(nx, 1)]
                    nc.vector.tensor_scalar(pre[0:N, KE:NB, 0:HALO], pre[0:N, KE:NB, SUP:SUP + HALO], kn, None,
                                            ALU.mult).then_inc(halo_done, 1)

                def keep_column(sec):
                    n = sec.n
                    dve.wait_ge(kept, FREE + n)
                    k = c["keep"][:, n:n + 1] if isinstance(n, int) else c["keep"][:, bass.ds(n, 1)]
                    nc.vector.tensor_scalar(kcol[:], ones[:, 0:1], k, None, ALU.mult).then_inc(kcol_ready, 1)

                def next_decays(sec):
                    n = sec.n
                    dve.wait_ge(hilo_ready, FREE + 2 * n)
                    nc.vector.tensor_scalar(aa[:, :, 0:H], a_step[:], FLOOR, None, ALU.max)
                    nc.vector.tensor_scalar(aa[:, :, 64:64 + H], a_step[:], FLOOR, -1.0, ALU.max, ALU.mult
                                            ).then_inc(aa_ready, 1)

                def next_xdt(sec):
                    n = sec.n
                    dve.wait_ge(ydiag_done, FREE + 2 * n * NS)
                    dve.wait_ge(xw_ready, FREE + 2 * n)
                    for j in range(2):
                        dve.wait_ge(xt_ready, FREE + 4 * n + 2 * j + 2)
                        nc.vector.tensor_tensor(xdt[:, j, :].rearrange("p (h q) -> p h q", h=H),
                                                xt[:, j, :].rearrange("p (h q) -> p h q", h=H),
                                                dt[:, j, :].unsqueeze(2).to_broadcast([P, H, HP]), ALU.mult
                                                ).then_inc(xdt_done, 1)

                def small(sec, j):
                    tile = 2 * sec.i + j
                    bank = sec.bank(f"small{j}")
                    dve.wait_ge(work_full, sec.full(f"small{j}"))
                    dve.wait_ge(e3_ready, FREE + tile)
                    nc.vector.tensor_copy(cs3[:].rearrange("p a h -> p (a h)"), bank[:, 0:3 * H]
                                          ).then_inc(cs3_ready, 1)
                    link(nc.vector.tensor_copy(gt[:], bank[:, 320:448]))
                    dve.wait_ge(lhs_ready, FREE + tile * cfg.chunks)
                    link(nc.vector.tensor_copy(hi[:], bank[:, 192:320]))
                    nc.vector.tensor_tensor(lo[:], bank[:, 192:320], hi[:].bitcast(F32), ALU.subtract
                                            ).then_inc(hilo_ready, 1)
                    dve.wait_ge(hilo_ready, FREE + tile + 1)
                    dve.wait_ge(exp_done, FREE + tile * NS)
                    for part, src in enumerate((hi, lo)):
                        ins = nc.vector.tensor_tensor(
                            c["rhs"][part][0:64], src[0:64].bitcast(F32).unsqueeze(1).to_broadcast([64, 4, P]),
                            c["in_head"][0:64].unsqueeze(2).to_broadcast([64, 4, P]), ALU.mult)
                    ins.then_inc(rhs_ready, 1)

                def from_state(sec, j):
                    tile = 2 * sec.i + j
                    for q in range(2):
                        name = f"yoff{j}" + "ab"[q]
                        dve.wait_ge(work_full, sec.full(name))
                        if q == 0:
                            if j == 0:
                                dve.wait_ge(kept, FREE + sec.i + 1)
                            dve.wait_ge(e3_ready, FREE + tile + 1)
                            dve.wait_ge(yy_done, FREE + tile)
                        hh = H // 2
                        nc.vector.tensor_tensor(y1[:, q * 512:(q + 1) * 512].rearrange("p (h q) -> p h q", h=hh),
                                                sec.bank(name)[:, :].rearrange("p (h q) -> p h q", h=hh),
                                                e3[:, 0, q * hh:(q + 1) * hh].unsqueeze(2).to_broadcast([P, hh, HP]),
                                                ALU.mult).then_inc(y1_ready, 1)

                def slot_mult(sec, j, s):
                    u = (2 * sec.i + j) * NS + s
                    dve.wait_ge(exp_done, FREE + u + 1)
                    nc.vector.tensor_tensor(decay[:, s % 2], decay[:, s % 2],
                                            gt[:].unsqueeze(1).to_broadcast([P, 8, P]), ALU.mult
                                            ).then_inc(m_ready, 1)

                def state_add(sec, j):
                    tile = 2 * sec.i + j
                    dve.wait_ge(dec_done, FREE + tile + 1)
                    for q in range(2):
                        name = f"state{j}" + "ab"[q]
                        dve.wait_ge(work_full, sec.full(name))
                        half = state[0:N, q * 512:(q + 1) * 512]
                        nc.vector.tensor_tensor(half, half, sec.bank(name)[0:N, :], ALU.add
                                                ).then_inc(state_ready, 1)

                def gate(sec, j):
                    tile = 2 * sec.i + j
                    dve.wait_ge(ydiag_done, FREE + NS * (tile + 1))
                    dve.wait_ge(y1x_ready, FREE + tile + 1)
                    dve.wait_ge(sq_done, FREE + tile)
                    nc.vector.tensor_tensor(yy[:], y1[:], ybank[:, :], ALU.add).then_inc(yy_done, 1)
                    dve.wait_ge(yy_done, FREE + tile + 1)
                    dve.wait_ge(zs_done, FREE + sec.i + 1)
                    dve.wait_ge(yzT_ready, FREE + 2 * tile)
                    nc.vector.tensor_tensor(yz[:], yy[:], zs[:, j, :], ALU.mult).then_inc(yz_done, 1)

                def rms_var(sec, j):
                    tile = 2 * sec.i + j
                    dve.wait_ge(sq_done, FREE + tile + 1)
                    nc.vector.tensor_scalar(rv[:], ss[:], 1.0 / E, cfg.eps, ALU.mult, ALU.add
                                            ).then_inc(rv_ready, 1)

                def out_add(sec, j):
                    tile = 2 * sec.i + j
                    dve.wait_ge(r1_ready, tile + 1)
                    newton_rsqrt(dve, nc, link, rr[:], rv[:], rt[:])
                    if j == 0:
                        dve.wait_ge(res_loaded, 16 * sec.i + 16)
                    dve.wait_ge(work_full, sec.full(f"out{j}"))
                    nc.vector.scalar_tensor_tensor(out=x_res[:, j, :], in0=sec.bank(f"out{j}")[:, :], scalar=rr[:],
                                                   in1=x_res[:, j, :], op0=ALU.mult, op1=ALU.add
                                                   ).then_inc(out_done, 1)

                def supertile(sec, with_next):
                    small(sec, 0)
                    if with_next:
                        dt_raw(sec)
                        dt_finish(sec)
                        fill = spread(list(range(NB)), NS)
                    else:
                        fill = [[]] * NS
                    from_state(sec, 0)
                    for s in range(NS):
                        slot_mult(sec, 0, s)
                        if fill[s]:
                            conv_blocks(sec, fill[s])
                    state_add(sec, 0)
                    small(sec, 1)
                    gate(sec, 0)
                    rms_var(sec, 0)
                    out_add(sec, 0)
                    from_state(sec, 1)
                    for s in range(NS):
                        slot_mult(sec, 1, s)
                    state_add(sec, 1)
                    gate(sec, 1)
                    if with_next:
                        next_decays(sec)
                        keep_column(sec)
                        halo(sec)
                    if sec.ln is not None:
                        norm_stats(sec.ln)
                    rms_var(sec, 1)
                    if sec.ln is not None:
                        norm_apply(sec.ln)
                    out_add(sec, 1)
                    if with_next:
                        next_xdt(sec)

                for s in (xn_ready, raw_ready, conv_done, halo_done, xdt_done, hilo_ready, y1_ready, state_ready,
                          yy_done, yz_done, out_done, rv_ready):
                    dve.sem_inc(s, FREE)
                dve.wait_ge(weights, cfg.weight_count)
                nc.vector.memset(aa[:], 0.0)
                nc.vector.memset(state[:], 0.0)
                nc.vector.memset(pre[:, :, 0:HALO], 0.0)
                link(nc.vector.tensor_scalar(a_low[:], a_log[:], 44.0, None, ALU.min))
                link(nc.vector.tensor_tensor(a_high[:], a_log[:], a_low[:], ALU.subtract))
                nc.vector.tensor_scalar(a_high[:], a_high[:], 80.0, None, ALU.min).then_inc(setup_v, 1)
                if cfg.conv_scale != 1.0:
                    for b, (_, m) in enumerate(cfg.blocks):
                        nc.vector.tensor_scalar(conv_w[0:m, b, :], conv_w[0:m, b, :], cfg.conv_scale, None, ALU.mult)
                for k in range(KE):
                    ins = nc.vector.tensor_scalar(w_out[:, k, :], w_out[:, k, :], norm_w[:, k:k + 1], None, ALU.mult)
                ins.then_inc(setup_v, 1)
                dve.wait_ge(setup_a, 1)
                dve.sem_inc(setup_v, 1)
                sec = prologue()
                norm_stats(0)
                norm_apply(0)
                dt_raw(sec)
                dt_finish(sec)
                for b in range(0, NB, 2):
                    conv_blocks(sec, [b, b + 1])
                next_decays(sec)
                keep_column(sec)
                halo(sec)
                norm_stats(1)
                norm_apply(1)
                next_xdt(sec)
                base = steps.section(0)
                per = 2 + 4 + 4 + 2 * 2 + 2 * NB + 2 * 4
                with dve.Fori(0, NSUP - 2) as i:
                    steps.section(i * per + base)
                    supertile(body(i), True)
                    assert steps.n == per, (steps.n, per)
                steps.section((NSUP - 2) * per + base)
                supertile(last_but_one(), True)
                supertile(last(), False)

            @block.gpsimd
            def _(pool):
                def operands(i, j):
                    tile = 2 * i + j
                    pool.wait_ge(hilo_ready, FREE + tile + 1)
                    pool.wait_ge(exp_done, FREE + tile * NS)
                    pool.wait_ge(dec_done, FREE + tile)
                    for ch in range(cfg.chunks):
                        for part, src in enumerate((hi, lo)):
                            g = slice(ch * CHG, (ch + 1) * CHG)
                            ins = nc.gpsimd.tensor_tensor(
                                c["lhs"][part][64:P, g, :],
                                src[64:P].bitcast(F32).unsqueeze(1).to_broadcast([64, CHG, P]),
                                c["in_group"][64:P, g].unsqueeze(2).to_broadcast([64, CHG, P]), ALU.mult)
                        ins.then_inc(lhs_ready, 1)

                def tile_steps(i, j, k):
                    tile = 2 * i + j
                    operands(i, j)
                    pool.wait_ge(lhs_ready, FREE + (tile + 1) * cfg.chunks)
                    pool.wait_ge(e3_ready, FREE + tile + 1)
                    if j == 0:
                        pool.wait_ge(kcol_ready, i + 1)
                        nc.gpsimd.tensor_tensor(e3[:, 0:3:2, :], e3[:, 0:3:2, :],
                                                kcol[:].unsqueeze(2).to_broadcast([P, 2, H]), ALU.mult
                                                ).then_inc(kept, 1)
                        pool.wait_ge(kept, FREE + i + 1)
                    pool.wait_ge(xt_ready, FREE + 4 * i + 2 * j + 2)
                    pool.wait_ge(sq_done, FREE + tile)
                    nc.gpsimd.tensor_tensor(skip[:].rearrange("p (h q) -> p h q", h=H),
                                            xt[:, j, :].rearrange("p (h q) -> p h q", h=H),
                                            d_skip[:].unsqueeze(2).to_broadcast([P, H, HP]), ALU.mult
                                            ).then_inc(p_chain, 1)
                    pool.wait_ge(y1_ready, FREE + 2 * tile + 2)
                    pool.wait_ge(p_chain, tile + 1)
                    nc.gpsimd.tensor_tensor(y1[:], y1[:], skip[:], ALU.add).then_inc(y1x_ready, 1)
                    pool.wait_ge(xdt_done, FREE + tile + 1)
                    pool.wait_ge(state_ready, FREE + 2 * tile)
                    nc.gpsimd.tensor_tensor(xw[:].rearrange("p (h q) -> p h q", h=H),
                                            xdt[:, j, :].rearrange("p (h q) -> p h q", h=H),
                                            e3[:, 1, :].unsqueeze(2).to_broadcast([P, H, HP]), ALU.mult
                                            ).then_inc(xw_ready, 1)
                    pool.wait_ge(xw_ready, FREE + tile + 1)
                    nc.gpsimd.tensor_tensor(state[0:N].rearrange("p (h q) -> p h q", h=H),
                                            state[0:N].rearrange("p (h q) -> p h q", h=H),
                                            e3[0:N, 2, :].unsqueeze(2).to_broadcast([N, H, HP]), ALU.mult
                                            ).then_inc(dec_done, 1)

                for s in (lhs_ready, y1x_ready, dec_done, kept, xw_ready):
                    pool.sem_inc(s, FREE)
                pool.wait_ge(weights, cfg.weight_count)
                with pool.Fori(0, NSUP) as i:
                    tile_steps(i, 0, None)
                    tile_steps(i, 1, None)

        clear_signals(nc, signals)


def ffn_phase(nc, tag, c, psum, x_src, x_dst, w):
    K_STEPS, HID = 4, 2048
    KH = HID // P
    NT = SEQ // P
    EPS = 1e-6
    ident = c["ident"]
    src_t = x_src.rearrange("(b t p) d -> b p t d", p=P, t=NT)
    dst_t = x_dst.rearrange("(b t p) d -> b p t d", p=P, t=NT)

    ctx = ExitStack()
    with ctx:
        def sb(name, shape, dt=F32):
            return ctx.enter_context(nc.sbuf_tensor(f"{tag}_{name}", shape, dt))

        signals = []

        def sig(name):
            signals.append(ctx.enter_context(nc.semaphore(f"{tag}_{name}")))
            return signals[-1]

        d1_w, d2_w = sb("d1_w", [P, KD, HID]), sb("d2_w", [P, KH, DM])
        agg_w, bc_w, gate_w = (sb(k, [P, KD, DM]) for k in ("agg_w", "bc_w", "gate_w"))
        in_gamma, in_beta = sb("in_gamma", [P, KD]), sb("in_beta", [P, KD])
        pn_gamma, pn_beta = sb("pn_gamma", [P, KD]), sb("pn_beta", [P, KD])
        agg_b, d2_b, d1_b = sb("agg_b", [P, KD]), sb("d2_b", [P, KD]), sb("d1_b", [P, KH])
        rows = {k: sb(f"{k}_row", [P, DM]) for k in ("gate_b", "bc_b", "out_gamma", "out_beta")}
        x_in, x_res = sb("x_in", [P, NT, DM]), sb("x_res", [P, NT, DM])
        x1, gate = sb("x1", [P, NT, DM]), sb("gate", [P, NT, DM])
        x1T = sb("x1T", [P, 2, KD, P])
        message, msg = sb("message", [P, BATCH, DM]), sb("msg", [P, DM])
        stats, mv = sb("stats", [P, NT, 6]), sb("mv", [P, NT, 2])
        v_in, r_in, t_in = sb("v_in", [P, NT]), sb("r_in", [P, NT]), sb("t_in", [P, NT])
        stats2, mv2 = sb("stats2", [P, NT, 6]), sb("mv2", [P, NT, 2])
        v_out, r_out = sb("v_out", [P, NT]), sb("r_out", [P, NT])
        carrier = sb("carrier", [P, 1])
        last = sb("last", [BATCH, DM])
        l_stats, l_mv = sb("l_stats", [BATCH, 6]), sb("l_mv", [BATCH, 2])
        l_v, l_r, l_t = sb("l_v", [BATCH, 1]), sb("l_r", [BATCH, 1]), sb("l_t", [BATCH, 1])
        th, cen, sq, tt = (sb(k, [P, KD, BATCH]) for k in ("th", "cen", "sq", "tt"))
        m_v, m_r, m_t = sb("m_v", [P, BATCH]), sb("m_r", [P, BATCH]), sb("m_t", [P, BATCH])
        hid = sb("hid", [P, KH, BATCH])

        seg, ybank, work = psum["seg"], psum["y"], psum["work"]
        hid_ps, col_ps = seg[0][:, 0:KH * BATCH], seg[0][:, 512:512 + KD * BATCH]
        mean_ps, var_ps = seg[1][:, 0:BATCH], seg[1][:, 512:512 + BATCH]
        msg_ps = [seg[k // 2][:, (k % 2) * 512:(k % 2 + 1) * 512] for k in range(BATCH)]

        vectors, w_agg, w_gate = sig("vectors"), sig("w_agg"), sig("w_gate")
        w_d1, w_d2, w_bc = sig("w_d1"), sig("w_d2"), sig("w_bc")
        last_loaded, x_loaded, res_loaded = sig("last_loaded"), sig("x_loaded"), sig("res_loaded")
        stored = sig("stored")
        v_chain = sig("v_chain")
        a_chain = sig("a_chain")
        rows_var, rows_r, rows_ready = sig("rows_var"), sig("rows_r"), sig("rows_ready")
        lastT_full, t_ready = sig("lastT_full"), sig("t_ready")
        col_full, th_ready = sig("col_full"), sig("th_ready")
        mean_full, sq_ready, var_full = sig("mean_full"), sig("sq_ready"), sig("var_full")
        mvar_ready, mr_ready = sig("mvar_ready"), sig("mr_ready")
        hid_full, pre_ready, hid_ready = sig("hid_full"), sig("pre_ready"), sig("hid_ready")
        msg_full, message_ready = sig("msg_full"), sig("message_ready")
        var_ready, r0_ready = sig("var_ready"), sig("r0_ready")
        x1_ready = sig("x1_ready")
        x1T_full, x1T_ready = sig("x1T_full"), sig("x1T_ready")
        gate_full = sig("gate_full")
        gate_raw = sig("gate_raw")
        gate_ready = sig("gate_ready")
        msg_ready = sig("msg_ready")
        gated = sig("gated")
        var2_ready, r2_ready = sig("var2_ready"), sig("r2_ready")
        normed = sig("normed")
        res_beta = sig("res_beta")
        scaled = sig("scaled")
        done = sig("done")

        with nc.Block() as block:
            @block.sync
            def _(sp):
                sp.sem_inc(stored, STORED)
                sp.dma_start(last[:], x_src.rearrange("(b s) d -> b s d", b=BATCH)[:, SEQ - 1, :]
                             ).then_inc(last_loaded, 16)
                count = 0
                with nc.allow_non_contiguous_dma(reason="small vectors"):
                    for dst, name in ((in_gamma, "in_gamma"), (in_beta, "in_beta"), (pn_gamma, "pn_gamma"),
                                      (pn_beta, "pn_beta"), (agg_b, "agg_b"), (d2_b, "d2_b"), (d1_b, "d1_b")):
                        sp.dma_start(dst[:], w[name].rearrange("(k p) -> p k", p=P)).then_inc(vectors, 16)
                        count += 16
                sp.dma_start(agg_w[:], w["agg_w"].rearrange("(k p) n -> p k n", p=P)).then_inc(w_agg, 16)
                for name, dst in rows.items():
                    sp.dma_start(dst[:], w[name].rearrange("(a d) -> a d", a=1).to_broadcast([P, DM])
                                 ).then_inc(vectors, 16)
                    count += 16
                c["vector_count"] = count
                sp.dma_start(d1_w[:], w["d1_w"].rearrange("(k p) n -> p k n", p=P)).then_inc(w_d1, 16)
                sp.dma_start(x_in[:], src_t[0]).then_inc(x_loaded, 16)
                sp.dma_start(gate_w[:], w["gate_w"].rearrange("(k p) n -> p k n", p=P)).then_inc(w_gate, 16)
                sp.dma_start(d2_w[:], w["d2_w"].rearrange("(k p) n -> p k n", p=P)).then_inc(w_d2, 16)
                sp.dma_start(bc_w[:], w["bc_w"].rearrange("(k p) n -> p k n", p=P)).then_inc(w_bc, 16)

                def step(b, n):
                    if n is not None:
                        sp.wait_ge(x1_ready, FREE + NT * n)
                        sp.dma_start(x_in[:], src_t[n]).then_inc(x_loaded, 16)
                    sp.wait_ge(stored, STORED + 32 * b)
                    sp.dma_start(x_res[:], src_t[b]).then_inc(res_loaded, 16)
                    for half in range(2):
                        t = slice(half * NT // 2, (half + 1) * NT // 2)
                        sp.wait_ge(done, FREE + NT * b + (half + 1) * NT // 2)
                        sp.dma_start(dst_t[b][:, t, :], x_res[:, t, :]).then_inc(stored, 16)

                with sp.Fori(0, BATCH - 1) as b:
                    step(b, b + 1)
                step(BATCH - 1, None)
                sp.wait_ge(stored, STORED + 32 * BATCH)

            @block.tensor
            def _(pe):
                def prepare(n, t):
                    pe.wait_ge(x1_ready, FREE + NT * n + t + 1)
                    pe.wait_ge(x1T_ready, FREE + NT * n + t - 1)
                    for k in range(KD):
                        mm = nc.tensor.transpose(work[t % 2][:, k * P:(k + 1) * P], x1[:, t, k * P:(k + 1) * P],
                                                 ident[:])
                    mm.then_inc(x1T_full, 1)

                def logits(n, t):
                    pe.wait_ge(x1T_ready, FREE + NT * n + t + 1)
                    pe.wait_ge(gate_raw, FREE + NT * n + t - 1)
                    for k in range(KD):
                        mm = nc.tensor.matmul(ybank[:, (t % 2) * 512:(t % 2 + 1) * 512], x1T[:, t % 2, k, :],
                                              gate_w[:, k, :], start=(k == 0), stop=(k == KD - 1))
                    mm.then_inc(gate_full, 1)

                def column(w_sb, cols, rhs, nk, out):
                    for m in range(cols):
                        for k in range(nk):
                            mm = nc.tensor.matmul(out[:, m * BATCH:(m + 1) * BATCH], w_sb[:, k, m * P:(m + 1) * P],
                                                  rhs[:, k, :], start=(k == 0), stop=(k == nk - 1))
                    return mm

                pe.sem_inc(gate_full, FREE)
                pe.wait_ge(rows_ready, 1)
                for k in range(KD):
                    mm = nc.tensor.matmul(col_ps[:, k * BATCH:(k + 1) * BATCH], last[:, k * P:(k + 1) * P],
                                          ident[0:BATCH, 0:BATCH], start=True, stop=True)
                mm.then_inc(lastT_full, 1)
                pe.wait_ge(t_ready, 1)
                pe.wait_ge(w_agg, 16)
                column(agg_w, KD, tt, KD, col_ps).then_inc(col_full, 1)
                for step in range(K_STEPS):
                    pe.wait_ge(th_ready, step + 1)
                    for k in range(KD):
                        mm = nc.tensor.matmul(mean_ps, c["mean_w"][:], th[:, k, :], start=(k == 0), stop=(k == KD - 1))
                    mm.then_inc(mean_full, 1)
                    if step == 0:
                        pe.wait_ge(w_gate, 16)
                    prepare(0, 2 * step)
                    pe.wait_ge(sq_ready, step + 1)
                    for k in range(KD):
                        mm = nc.tensor.matmul(var_ps, c["mean_w"][:], sq[:, k, :], start=(k == 0), stop=(k == KD - 1))
                    mm.then_inc(var_full, 1)
                    logits(0, 2 * step)
                    pe.wait_ge(t_ready, step + 2)
                    if step == 0:
                        pe.wait_ge(w_d1, 16)
                    column(d1_w, KH, tt, KD, hid_ps).then_inc(hid_full, 1)
                    prepare(0, 2 * step + 1)
                    logits(0, 2 * step + 1)
                    pe.wait_ge(hid_ready, step + 1)
                    if step == 0:
                        pe.wait_ge(w_d2, 16)
                    column(d2_w, KD, hid, KH, col_ps).then_inc(col_full, 1)
                pe.wait_ge(th_ready, K_STEPS + 1)
                pe.wait_ge(w_bc, 16)
                for b in range(BATCH):
                    for k in range(KD):
                        mm = nc.tensor.matmul(msg_ps[b], th[:, k, b:b + 1].to_broadcast([P, P]), bc_w[:, k, :],
                                              start=(k == 0), stop=(k == KD - 1))
                    mm.then_inc(msg_full, 1)

                def batch(n):
                    prepare(n, 0)
                    for t in range(NT):
                        if t + 1 < NT:
                            prepare(n, t + 1)
                        logits(n, t)

                with pe.Fori(0, BATCH - 1) as b:
                    batch(b + 1)

            @block.scalar
            def _(act):
                steps = Steps()

                def link(ins):
                    ins.then_inc(a_chain, 1)
                    act.wait_ge(a_chain, steps.next())

                def rsqrt(r, v, out_signal):
                    link(nc.scalar.activation(r, v, ACT.Ln))
                    nc.scalar.activation(r, r, ACT.Exp, scale=-0.5).then_inc(out_signal, 1)

                def x1T_copy(n, t):
                    act.wait_ge(x1T_full, NT * n + t + 1)
                    act.wait_ge(gate_full, FREE + NT * n + t - 1)
                    nc.scalar.copy(x1T[:, t % 2], work[t % 2][:, :].rearrange("p (k q) -> p k q", k=KD)
                                   ).then_inc(x1T_ready, 1)

                def sigmoid(n, t):
                    act.wait_ge(gate_raw, FREE + NT * n + t + 1)
                    nc.scalar.activation(gate[:, t, :], gate[:, t, :], ACT.Sigmoid).then_inc(gate_ready, 1)

                act.sem_inc(x1T_ready, FREE)
                act.wait_ge(rows_var, 1)
                rsqrt(l_r[:], l_v[:], rows_r)
                act.wait_ge(rows_var, 2)
                rsqrt(l_r[:], l_v[:], rows_r)
                act.wait_ge(var_ready, 1)
                rsqrt(r_in[:], v_in[:], r0_ready)
                for step in range(K_STEPS):
                    x1T_copy(0, 2 * step)
                    act.wait_ge(mvar_ready, step + 1)
                    rsqrt(m_r[:], m_v[:], mr_ready)
                    act.wait_ge(pre_ready, step + 1)
                    nc.scalar.activation(hid[:], hid[:], ACT.Gelu).then_inc(hid_ready, 1)
                    x1T_copy(0, 2 * step + 1)
                for t in range(NT):
                    sigmoid(0, t)

                def batch(b, n):
                    act.wait_ge(var2_ready, b + 1)
                    rsqrt(r_out[:], v_out[:], r2_ready)
                    if n is not None:
                        act.wait_ge(var_ready, n + 1)
                        rsqrt(r_in[:], v_in[:], r0_ready)
                        for t in range(NT):
                            x1T_copy(n, t)
                            if t:
                                sigmoid(n, t - 1)
                        sigmoid(n, NT - 1)

                base = steps.section(0)
                with act.Fori(0, BATCH - 1) as b:
                    steps.section(b * 2 + base)
                    batch(b, b + 1)
                    assert steps.n == 2
                steps.section((BATCH - 1) * 2 + base)
                batch(BATCH - 1, None)

            @block.vector
            def _(dve):
                steps = Steps()

                def link(ins):
                    ins.then_inc(v_chain, 1)
                    dve.wait_ge(v_chain, steps.next())

                def over_k(vec):
                    return vec[:].unsqueeze(1).to_broadcast([P, KD, BATCH])

                def over_b(vec, blocks=KD):
                    return vec[:].unsqueeze(2).to_broadcast([P, blocks, BATCH])

                def normalise_last(k, eps):
                    link(nc.vector.bn_stats(l_stats[:], last[:]))
                    link(nc.vector.bn_aggr(l_mv[:], l_stats[:]))
                    nc.vector.tensor_scalar(l_v[:], l_mv[:, 1:2], eps, None, ALU.add).then_inc(rows_var, 1)
                    dve.wait_ge(rows_r, k + 1)
                    newton_rsqrt(dve, nc, link, l_r[:], l_v[:], l_t[:])
                    ins = nc.vector.tensor_scalar(last[:], last[:], l_mv[:, 0:1], l_r[:], ALU.subtract, ALU.mult)
                    if k:
                        ins.then_inc(rows_ready, 1)
                    else:
                        link(ins)

                def statistics(n):
                    dve.wait_ge(x_loaded, 16 * n + 16)
                    for t in range(NT):
                        ins = nc.vector.bn_stats(stats[:, t, :], x_in[:, t, :])
                    link(ins)
                    nc.vector.memset(carrier[:], 0.0)
                    for t in range(NT):
                        ins = nc.vector.bn_aggr(mv[:, t, :], stats[:, t, :])
                    link(ins)
                    nc.vector.tensor_scalar(v_in[:], mv[:, :, 1], LN_EPS, None, ALU.add
                                            ).then_inc(var_ready, 1)

                def scale_in(n):
                    dve.wait_ge(r0_ready, n + 1)
                    newton_rsqrt(dve, nc, link, r_in[:], v_in[:], t_in[:])

                def make_x1(n, t):
                    nc.vector.tensor_scalar(x1[:, t, :], x_in[:, t, :], mv[:, t, 0:1], r_in[:, t:t + 1],
                                            ALU.subtract, ALU.mult).then_inc(x1_ready, 1)

                def add_gate_bias(n, t):
                    dve.wait_ge(gate_full, FREE + NT * n + t + 1)
                    if t == 0:
                        dve.wait_ge(done, FREE + NT * n)
                    nc.vector.tensor_tensor(gate[:, t, :], ybank[:, (t % 2) * 512:(t % 2 + 1) * 512],
                                            rows["gate_b"][:], ALU.add).then_inc(gate_raw, 1)

                for s in (x1_ready, gate_raw, done):
                    dve.sem_inc(s, FREE)
                dve.wait_ge(last_loaded, 16)
                normalise_last(0, LN_EPS)
                normalise_last(1, EPS)
                dve.wait_ge(lastT_full, 1)
                dve.wait_ge(vectors, c["vector_count"])
                col3 = col_ps.rearrange("p (k b) -> p k b", k=KD)
                link(nc.vector.tensor_tensor(tt[:], col3, over_b(in_gamma), ALU.mult))
                nc.vector.tensor_tensor(tt[:], tt[:], over_b(in_beta), ALU.add).then_inc(t_ready, 1)
                statistics(0)
                scale_in(0)
                dve.wait_ge(col_full, 1)
                nc.vector.tensor_tensor(th[:], col3, over_b(agg_b), ALU.add).then_inc(th_ready, 1)
                for t in range(NT):
                    make_x1(0, t)
                for step in range(K_STEPS):
                    dve.wait_ge(mean_full, step + 1)
                    dve.wait_ge(th_ready, step + 1)
                    link(nc.vector.scalar_tensor_tensor(out=cen[:], in0=mean_ps.unsqueeze(1).to_broadcast(
                        [P, KD, BATCH]), scalar=-1.0, in1=th[:], op0=ALU.mult, op1=ALU.add))
                    nc.vector.tensor_tensor(sq[:], cen[:], cen[:], ALU.mult).then_inc(sq_ready, 1)
                    dve.wait_ge(var_full, step + 1)
                    nc.vector.tensor_scalar(m_v[:], var_ps, EPS, None, ALU.add).then_inc(mvar_ready, 1)
                    dve.wait_ge(mr_ready, step + 1)
                    newton_rsqrt(dve, nc, link, m_r[:], m_v[:], m_t[:])
                    link(nc.vector.tensor_tensor(cen[:], cen[:], over_k(m_r), ALU.mult))
                    link(nc.vector.tensor_tensor(tt[:], cen[:], over_b(pn_gamma), ALU.mult))
                    nc.vector.tensor_tensor(tt[:], tt[:], over_b(pn_beta), ALU.add).then_inc(t_ready, 1)
                    add_gate_bias(0, 2 * step)
                    dve.wait_ge(hid_full, step + 1)
                    nc.vector.tensor_tensor(hid[:], hid_ps.rearrange("p (k b) -> p k b", k=KH),
                                            over_b(d1_b, KH), ALU.add).then_inc(pre_ready, 1)
                    add_gate_bias(0, 2 * step + 1)
                    link(nc.vector.tensor_tensor(th[:], th[:], over_b(d2_b), ALU.add))
                    dve.wait_ge(col_full, step + 2)
                    nc.vector.tensor_tensor(th[:], th[:], col3, ALU.add).then_inc(th_ready, 1)
                for b in range(BATCH):
                    dve.wait_ge(msg_full, b + 1)
                    nc.vector.tensor_tensor(message[:, b, :], msg_ps[b], rows["bc_b"][:], ALU.add
                                            ).then_inc(message_ready, 1)
                dve.wait_ge(message_ready, BATCH)

                def batch(b, n):
                    now = message[:, b, :] if isinstance(b, int) else \
                        message[:].rearrange("p b d -> p (b d)")[:, bass.ds(b * DM, DM)]
                    dve.wait_ge(gated, FREE + NT * b)
                    nc.vector.tensor_scalar(msg[:], now, 1.0, None, ALU.mult).then_inc(msg_ready, 1)
                    for t in range(NT):
                        dve.wait_ge(gated, FREE + NT * b + t + 1)
                        ins = nc.vector.tensor_tensor(x1[:, t, :], x1[:, t, :], gate[:, t, :], ALU.add)
                        if t == NT - 1:
                            link(ins)
                    for t in range(NT):
                        ins = nc.vector.bn_stats(stats2[:, t, :], x1[:, t, :])
                    link(ins)
                    nc.vector.memset(carrier[:], 0.0)
                    for t in range(NT):
                        ins = nc.vector.bn_aggr(mv2[:, t, :], stats2[:, t, :])
                    link(ins)
                    nc.vector.tensor_scalar(v_out[:], mv2[:, :, 1], EPS, None, ALU.add
                                            ).then_inc(var2_ready, 1)
                    if n is not None:
                        statistics(n)
                    dve.wait_ge(r2_ready, b + 1)
                    newton_rsqrt(dve, nc, link, r_out[:], v_out[:], t_in[:])
                    for t in range(NT):
                        nc.vector.tensor_scalar(gate[:, t, :], x1[:, t, :], mv2[:, t, 0:1], r_out[:, t:t + 1],
                                                ALU.subtract, ALU.mult).then_inc(normed, 1)
                    if n is not None:
                        scale_in(n)
                        for t in range(NT):
                            if t == 0:
                                dve.wait_ge(normed, NT * n)
                            make_x1(n, t)
                    for t in range(NT):
                        dve.wait_ge(scaled, NT * b + t + 1)
                        dve.wait_ge(res_beta, NT * b + t + 1)
                        nc.vector.tensor_tensor(x_res[:, t, :], x_res[:, t, :], gate[:, t, :], ALU.add
                                                ).then_inc(done, 1)
                    if n is not None:
                        for t in range(NT):
                            add_gate_bias(n, t)

                base = steps.section(0)
                per = 3 + 2 + 4 + 4
                with dve.Fori(0, BATCH - 1) as b:
                    steps.section(b * per + base)
                    batch(b, b + 1)
                    assert steps.n == per, steps.n
                steps.section((BATCH - 1) * per + base)
                batch(BATCH - 1, None)

            @block.gpsimd
            def _(pool):
                pool.sem_inc(gated, FREE)
                pool.wait_ge(vectors, c["vector_count"])
                with pool.Fori(0, BATCH) as b:
                    pool.wait_ge(msg_ready, b + 1)
                    for t in range(NT):
                        pool.wait_ge(gate_ready, NT * b + t + 1)
                        nc.gpsimd.tensor_tensor(gate[:, t, :], gate[:, t, :], msg[:], ALU.mult
                                                ).then_inc(gated, 1)
                    pool.wait_ge(res_loaded, 16 * b + 16)
                    for t in range(NT):
                        nc.gpsimd.tensor_tensor(x_res[:, t, :], x_res[:, t, :], rows["out_beta"][:], ALU.add
                                                ).then_inc(res_beta, 1)
                    for t in range(NT):
                        pool.wait_ge(normed, NT * b + t + 1)
                        nc.gpsimd.tensor_tensor(gate[:, t, :], gate[:, t, :], rows["out_gamma"][:], ALU.mult
                                                ).then_inc(scaled, 1)

        clear_signals(nc, signals)


STAGES = "AFBF"


def build(nc, out, **a):
    x_mid = [nc.dram_tensor(f"x_mid{k}", (TOK, DM), F32).ap() for k in range(3)]
    x0 = a["L0_attn_a_x"].rearrange("b s d -> (b s) d")
    y = out.rearrange("b s d -> (b s) d")
    mixer_a = Mixer("a", heads=16, head_dim=64, state=64, eps=1e-6, gate_scale=1.0, conv_scale=1.0, gate_first=True)
    mixer_b = Mixer("b", heads=64, head_dim=16, state=128, eps=1e-5, gate_scale=0.25, conv_scale=0.5,
                    gate_first=False)

    def part(prefix):
        return {k[len(prefix):].removesuffix("_w") if k.endswith("proj_w") else k[len(prefix):]: v
                for k, v in a.items() if k.startswith(prefix)}

    with ExitStack() as ctx:
        psum = {
            "work": [ctx.enter_context(nc.psum_tensor(f"work{k}", [P, 512], F32)) for k in range(2)],
            "seg": [ctx.enter_context(nc.psum_tensor(f"seg{k}", [P, 1024], F32)) for k in range(2)],
            "y": ctx.enter_context(nc.psum_tensor("y", [P, 1024], F32)),
        }
        c = build_constants(nc, ctx)
        route = [x0] + x_mid[:len(STAGES) - 1] + [y]
        for k, stage in enumerate(STAGES):
            src, dst = route[k], route[k + 1]
            if stage == "A":
                mixer_phase(nc, mixer_a, c, None, psum, src, dst, part("L0_attn_a_"))
            elif stage == "B":
                mixer_phase(nc, mixer_b, c, None, psum, src, dst, part("L0_attn_b_"))
            else:
                ffn_phase(nc, f"f{k}", c, psum, src, dst, part("L0_ffn_"))


_OUTS = [((BATCH, SEQ, DM), "float32")]


def kernel(**inputs):
    import numpy as _np
    import concourse.bacc as _bacc
    from concourse import mybir as _mybir
    from concourse.bass_utils import run_bass_kernel_spmd as _run

    nc = _bacc.Bacc("TRN2", target_bir_lowering=False, num_devices=1)
    arrays, args = {}, {}
    for name, value in inputs.items():
        v = _np.asarray(value)
        if name in ("L0_attn_a_in_proj_w", "L0_attn_a_out_proj_w"):
            v = v.T
        v = _np.ascontiguousarray(v)
        arrays[f"in_{name}"] = v
        args[name] = nc.dram_tensor(f"in_{name}", v.shape, _mybir.dt.from_np(v.dtype), kind="ExternalInput").ap()
    shape, dtype = _OUTS[0]
    out = nc.dram_tensor("out_0", shape, _mybir.dt.from_np(_np.dtype(dtype)), kind="ExternalOutput").ap()
    build(nc, out, **args)
    r = _run(nc, [arrays], core_ids=[0])
    return r.results[0]["out_0"]
```
